# Optimizing a Trainium2 kernel written in Bass

```python
import numpy as np
import jax
import jax.numpy as jnp

def _softmax(x, axis=-1):
    return jax.nn.softmax(x, axis=axis)

def _gelu(x):
    return jax.nn.gelu(x, approximate=True)

def _silu(x):
    return jax.nn.silu(x)

def _sigmoid(x):
    return jax.nn.sigmoid(x)

def _layernorm(x, axis=-1, eps=1e-05):
    m = jnp.mean(x, axis=axis, keepdims=True)
    v = jnp.var(x, axis=axis, keepdims=True)
    return (x - m) / jnp.sqrt(v + eps)

def _scatter_add(tgt, idx, src, axis=0):
    return tgt.at[idx].add(src)

def _segment_sum(src, seg, n):
    return jax.ops.segment_sum(src, seg, n)
kernel_name = 'mk_hybrid_d1_jaxref_r4_f223ac'

def setup_inputs(seed: int=0):
    np.random.seed(seed)
    _w = jnp.asarray

    def _L0_attn_a_setup():
        import jax, jax.numpy as jnp
        import numpy as np
        import math
        HIDDEN = 512
        HEADS = 16
        HEAD_DIM = HIDDEN // HEADS
        SEQ = 512
        BATCH = 1
        THRESH = 0.7
        key = jax.random.key(seed)
        ks = jax.random.split(key, 9)
        init = lambda k, shape: jax.random.normal(k, shape, dtype=jnp.float32) * 0.02
        return {'hidden_states': jax.random.normal(ks[0], (BATCH, SEQ, HIDDEN), dtype=jnp.float32), 'Wq': init(ks[1], (HIDDEN, HIDDEN)), 'bq': jnp.zeros((HIDDEN,), jnp.float32), 'Wk': init(ks[2], (HIDDEN, HIDDEN)), 'bk': jnp.zeros((HIDDEN,), jnp.float32), 'Wv': init(ks[3], (HIDDEN, HIDDEN)), 'bv': jnp.zeros((HIDDEN,), jnp.float32), 'Wo': init(ks[4], (HIDDEN, HIDDEN)), 'bo': jnp.zeros((HIDDEN,), jnp.float32), 'truth_gate': jnp.full((1,), THRESH, jnp.float32), 'balance_gate': jnp.full((1,), THRESH, jnp.float32), 'order_gate': jnp.full((1,), THRESH, jnp.float32), 'justice_gate': jnp.full((1,), THRESH, jnp.float32), 'harmony_gate': jnp.full((1,), THRESH, jnp.float32)}
    _L0_attn_a_in = _L0_attn_a_setup()

    def _L0_attn_b_setup():
        import jax, jax.numpy as jnp
        import numpy as np
        B_, L_, D_MODEL = (2, 1024, 512)
        EXPAND, HEADDIM, DCONV = (2, 64, 4)
        INNER = EXPAND * D_MODEL
        NHEADS = INNER // HEADDIM
        key = jax.random.key(seed)
        ks = jax.random.split(key, 8)
        f32 = jnp.float32
        return {'hidden_states': jax.random.normal(ks[0], (B_, L_, D_MODEL), f32), 'in_proj_w': jax.random.normal(ks[1], (INNER, D_MODEL), f32) * 0.02, 'gate_proj_w': jax.random.normal(ks[2], (INNER, D_MODEL), f32) * 0.02, 'out_proj_w': jax.random.normal(ks[3], (D_MODEL, INNER), f32) * 0.02, 'conv_w': jax.random.normal(ks[4], (INNER, DCONV), f32) * 0.02, 'conv_b': jnp.zeros((INNER,), f32), 'dt_w': jax.random.normal(ks[5], (NHEADS, HEADDIM), f32) * 0.02, 'dt_b': jnp.zeros((NHEADS,), f32), 'A_log': jnp.zeros((NHEADS, HEADDIM), f32), 'Bp': jax.random.normal(ks[6], (NHEADS, HEADDIM), f32) * 0.02, 'Cp': jax.random.normal(ks[7], (NHEADS, HEADDIM), f32) * 0.02, 'Dp': jnp.ones((NHEADS, HEADDIM), f32)}
    _L0_attn_b_in = _L0_attn_b_setup()

    def _L0_ffn_setup():
        import jax, jax.numpy as jnp
        import numpy as np
        B, S, H, I = (1, 64, 512, 1536)

        def _quantized_matmul(x, w, scale):
            wq = w.astype(jnp.float8_e4m3fn).astype(x.dtype)
            y = jnp.einsum('bsi,io->bso', x, wq)
            return y * scale
        key = jax.random.key(seed)
        ks = jax.random.split(key, 7)
        return {'x': jax.random.normal(ks[0], (B, S, H), dtype=jnp.float32), 'gate_w': jax.random.normal(ks[1], (H, I), dtype=jnp.float32) * 0.02, 'up_w': jax.random.normal(ks[2], (H, I), dtype=jnp.float32) * 0.02, 'down_w': jax.random.normal(ks[3], (I, H), dtype=jnp.float32) * 0.02, 'gate_scale': jax.random.uniform(ks[4], (I,), dtype=jnp.float32, minval=0.5, maxval=1.5), 'up_scale': jax.random.uniform(ks[5], (I,), dtype=jnp.float32, minval=0.5, maxval=1.5), 'down_scale': jax.random.uniform(ks[6], (H,), dtype=jnp.float32, minval=0.5, maxval=1.5)}
    _L0_ffn_in = _L0_ffn_setup()
    _d = {'L0_attn_a_hidden_states': _L0_attn_a_in['hidden_states'], 'L0_attn_a_Wq': _L0_attn_a_in['Wq'], 'L0_attn_a_bq': _L0_attn_a_in['bq'], 'L0_attn_a_Wk': _L0_attn_a_in['Wk'], 'L0_attn_a_bk': _L0_attn_a_in['bk'], 'L0_attn_a_Wv': _L0_attn_a_in['Wv'], 'L0_attn_a_bv': _L0_attn_a_in['bv'], 'L0_attn_a_Wo': _L0_attn_a_in['Wo'], 'L0_attn_a_bo': _L0_attn_a_in['bo'], 'L0_attn_a_truth_gate': _L0_attn_a_in['truth_gate'], 'L0_attn_a_balance_gate': _L0_attn_a_in['balance_gate'], 'L0_attn_a_order_gate': _L0_attn_a_in['order_gate'], 'L0_attn_a_justice_gate': _L0_attn_a_in['justice_gate'], 'L0_attn_a_harmony_gate': _L0_attn_a_in['harmony_gate'], 'L0_attn_b_in_proj_w': _L0_attn_b_in['in_proj_w'], 'L0_attn_b_gate_proj_w': _L0_attn_b_in['gate_proj_w'], 'L0_attn_b_out_proj_w': _L0_attn_b_in['out_proj_w'], 'L0_attn_b_conv_w': _L0_attn_b_in['conv_w'], 'L0_attn_b_conv_b': _L0_attn_b_in['conv_b'], 'L0_attn_b_dt_w': _L0_attn_b_in['dt_w'], 'L0_attn_b_dt_b': _L0_attn_b_in['dt_b'], 'L0_attn_b_A_log': _L0_attn_b_in['A_log'], 'L0_attn_b_Bp': _L0_attn_b_in['Bp'], 'L0_attn_b_Cp': _L0_attn_b_in['Cp'], 'L0_attn_b_Dp': _L0_attn_b_in['Dp'], 'L0_ffn_gate_w': _L0_ffn_in['gate_w'], 'L0_ffn_up_w': _L0_ffn_in['up_w'], 'L0_ffn_down_w': _L0_ffn_in['down_w'], 'L0_ffn_gate_scale': _L0_ffn_in['gate_scale'], 'L0_ffn_up_scale': _L0_ffn_in['up_scale'], 'L0_ffn_down_scale': _L0_ffn_in['down_scale']}
    _x0 = _d['L0_attn_a_hidden_states']
    _d['L0_attn_a_hidden_states'] = jax.random.normal(jax.random.fold_in(jax.random.key(seed), 1), (4, 512, 512), dtype=_x0.dtype)
    del _x0
    return _d

def reference(L0_attn_a_hidden_states, L0_attn_a_Wq, L0_attn_a_bq, L0_attn_a_Wk, L0_attn_a_bk, L0_attn_a_Wv, L0_attn_a_bv, L0_attn_a_Wo, L0_attn_a_bo, L0_attn_a_truth_gate, L0_attn_a_balance_gate, L0_attn_a_order_gate, L0_attn_a_justice_gate, L0_attn_a_harmony_gate, L0_attn_b_in_proj_w, L0_attn_b_gate_proj_w, L0_attn_b_out_proj_w, L0_attn_b_conv_w, L0_attn_b_conv_b, L0_attn_b_dt_w, L0_attn_b_dt_b, L0_attn_b_A_log, L0_attn_b_Bp, L0_attn_b_Cp, L0_attn_b_Dp, L0_ffn_gate_w, L0_ffn_up_w, L0_ffn_down_w, L0_ffn_gate_scale, L0_ffn_up_scale, L0_ffn_down_scale):

    def _L0_attn_a_ref(hidden_states, Wq, bq, Wk, bk, Wv, bv, Wo, bo, truth_gate, balance_gate, order_gate, justice_gate, harmony_gate):
        import jax, jax.numpy as jnp
        import numpy as np
        import math
        HIDDEN = 512
        HEADS = 16
        HEAD_DIM = HIDDEN // HEADS
        SEQ = 512
        BATCH = 1
        THRESH = 0.7
        B, S, D = hidden_states.shape
        H, hd = (HEADS, HEAD_DIM)

        def proj(W, b):
            return (hidden_states @ W.T + b).reshape(B, S, H, hd).transpose(0, 2, 1, 3)
        q, k, v = (proj(Wq, bq), proj(Wk, bk), proj(Wv, bv))
        scores = jnp.einsum('bhqd,bhkd->bhqk', q, k) / math.sqrt(hd)
        truth_penalty = jax.nn.sigmoid(truth_gate) * (jnp.linalg.norm(k, axis=-1, keepdims=True) * 0.01)
        logp = jax.nn.log_softmax(scores, axis=-1)
        entropy = -jnp.sum(jnp.exp(logp) * logp, axis=-1, keepdims=True)
        balance_adjustment = jax.nn.sigmoid(balance_gate) * (entropy / math.log(S) * 0.1)
        position_bias = jnp.arange(S, dtype=jnp.float32) / S
        order_bonus = jax.nn.sigmoid(order_gate) * (position_bias * 0.05)
        mean_score = scores.mean(axis=-1, keepdims=True)
        justice_adjustment = jax.nn.sigmoid(justice_gate) * ((mean_score - scores) * 0.1)
        smoothness = -jnp.abs(scores[..., 1:] - scores[..., :-1]).mean(axis=-1, keepdims=True)
        harmony_smooth = jax.nn.sigmoid(harmony_gate) * (smoothness * 0.1)
        scores = scores - truth_penalty + balance_adjustment + order_bonus + justice_adjustment + harmony_smooth
        attn = jax.nn.softmax(scores, axis=-1)
        out = jnp.einsum('bhqk,bhkd->bhqd', attn, v)
        out = out.transpose(0, 2, 1, 3).reshape(B, S, D)
        return out @ Wo.T + bo

    def _L0_attn_b_ref(hidden_states, in_proj_w, gate_proj_w, out_proj_w, conv_w, conv_b, dt_w, dt_b, A_log, Bp, Cp, Dp):
        import jax, jax.numpy as jnp
        import numpy as np
        B_, L_, D_MODEL = (2, 1024, 512)
        EXPAND, HEADDIM, DCONV = (2, 64, 4)
        INNER = EXPAND * D_MODEL
        NHEADS = INNER // HEADDIM
        B, L, _ = hidden_states.shape
        proj = hidden_states @ in_proj_w.T
        gate = jax.nn.sigmoid(hidden_states @ gate_proj_w.T)
        xp = jnp.pad(proj, ((0, 0), (DCONV - 1, 0), (0, 0)))
        conv = conv_b
        for k in range(DCONV):
            conv = conv + xp[:, k:k + L, :] * conv_w[:, k]
        conv = jax.nn.silu(conv)
        X = conv.reshape(B, L, NHEADS, HEADDIM)
        dt = jnp.einsum('blhp,hp->blh', X, dt_w) + dt_b
        dt = jax.nn.softplus(dt)
        A = -jnp.exp(A_log)
        decay = jnp.exp(dt[..., None] * A)
        drive = dt[..., None] * Bp * X

        def step(s, xs):
            d_t, b_t = xs
            s = d_t * s + b_t
            return (s, s)
        s0 = jnp.zeros((B, NHEADS, HEADDIM), X.dtype)
        _, states = jax.lax.scan(step, s0, (jnp.moveaxis(decay, 1, 0), jnp.moveaxis(drive, 1, 0)))
        states = jnp.moveaxis(states, 0, 1)
        y = Cp * states + Dp * X
        combined = y.reshape(B, L, INNER) * gate
        return combined @ out_proj_w.T

    def _L0_ffn_ref(x, gate_w, up_w, down_w, gate_scale, up_scale, down_scale):
        import jax, jax.numpy as jnp
        import numpy as np
        B, S, H, I = (1, 64, 512, 1536)

        def _quantized_matmul(x, w, scale):
            wq = w.astype(jnp.float8_e4m3fn).astype(x.dtype)
            y = jnp.einsum('bsi,io->bso', x, wq)
            return y * scale
        gate = jax.nn.silu(_quantized_matmul(x, gate_w, gate_scale))
        up = _quantized_matmul(x, up_w, up_scale)
        fuse = gate * up
        return _quantized_matmul(fuse, down_w, down_scale)
    x = L0_attn_a_hidden_states
    x = x + _L0_attn_a_ref(_layernorm(x, axis=-1), L0_attn_a_Wq, L0_attn_a_bq, L0_attn_a_Wk, L0_attn_a_bk, L0_attn_a_Wv, L0_attn_a_bv, L0_attn_a_Wo, L0_attn_a_bo, L0_attn_a_truth_gate, L0_attn_a_balance_gate, L0_attn_a_order_gate, L0_attn_a_justice_gate, L0_attn_a_harmony_gate)
    x = x + _L0_ffn_ref(_layernorm(x, axis=-1), L0_ffn_gate_w, L0_ffn_up_w, L0_ffn_down_w, L0_ffn_gate_scale, L0_ffn_up_scale, L0_ffn_down_scale)
    x = x + _L0_attn_b_ref(_layernorm(x, axis=-1), L0_attn_b_in_proj_w, L0_attn_b_gate_proj_w, L0_attn_b_out_proj_w, L0_attn_b_conv_w, L0_attn_b_conv_b, L0_attn_b_dt_w, L0_attn_b_dt_b, L0_attn_b_A_log, L0_attn_b_Bp, L0_attn_b_Cp, L0_attn_b_Dp)
    x = x + _L0_ffn_ref(_layernorm(x, axis=-1), L0_ffn_gate_w, L0_ffn_up_w, L0_ffn_down_w, L0_ffn_gate_scale, L0_ffn_up_scale, L0_ffn_down_scale)
    return x

_drawn_inputs = setup_inputs


def setup_inputs(seed=0):
    import zlib

    import numpy as np

    out = dict(_drawn_inputs(seed))
    spreads = {'L0_attn_a_bq': (0.0, 0.8),
     'L0_attn_a_bk': (0.0, 2.0),
     'L0_attn_a_bv': (0.0, 0.1),
     'L0_attn_a_bo': (0.0, 0.1),
     'L0_attn_b_conv_b': (0.0, 0.494),
     'L0_attn_b_dt_b': (0.0, 2.0),
     'L0_attn_b_A_log': (0.0, 2.0),
     'L0_attn_b_Dp': (1.0, 0.6)}
    factors = {'L0_attn_a_Wq': 8.0,
     'L0_attn_a_Wk': 8.0,
     'L0_attn_a_Wv': 5.942,
     'L0_attn_b_in_proj_w': 8.0,
     'L0_attn_b_gate_proj_w': 8.0,
     'L0_attn_b_out_proj_w': 3.541,
     'L0_attn_b_conv_w': 8.0,
     'L0_attn_b_dt_w': 34.246,
     'L0_attn_b_Bp': 8.0,
     'L0_attn_b_Cp': 8.0}
    for name, (base, spread) in spreads.items():
        noise = np.random.default_rng([zlib.crc32(name.encode()), seed]).standard_normal(out[name].shape)
        drawn = base * np.exp(spread * noise) if base else spread * noise
        out[name] = jnp.asarray(drawn.astype(out[name].dtype))
    for name, factor in factors.items():
        out[name] = (out[name] * factor).astype(out[name].dtype)
    return out
```

```python
from contextlib import ExitStack, contextmanager
import math

import concourse.bass as bass
from concourse import mybir

F32 = mybir.dt.float32
F32R = mybir.dt.float32r
I32 = mybir.dt.int32
FP8 = mybir.dt.float8e4
BF16 = mybir.dt.bfloat16
ALU = mybir.AluOpType
ACT = mybir.ActivationFunctionType
AX = mybir.AxisListType.X

P = 128
BATCH, SEQ, DM = 4, 512, 512
HEADS, HD = 16, 32
TT = SEQ // P
KT = DM // P
HG = P // HD
GROUPS = HEADS // HG
GT = HG * TT
NS = HEADS * TT
FF = 1536
FT = FF // P
INNER, HDIM, DCONV = 1024, 64, 4
MT = INNER // P
EPS = 1e-5
ORDER_STEP = 0.05 / SEQ

KSTK = 3 * HD
ROW_R = KSTK
ROW_O = KSTK + 2
KALL = KSTK + 4
LAG = 24

COLS = {}
_at = 0
for _n, _w in (("bq", KT), ("bk", KT), ("bv", KT), ("gate_scale", FT), ("up_scale", FT), ("conv_w", MT * DCONV),
               ("conv_b", MT), ("dt_w", MT), ("dt_b", MT), ("A_log", MT), ("Bp", MT), ("Cp", MT),
               ("Dp", MT), ("gates", 5)):
    COLS[_n] = _at
    _at += _w
NCOL = _at


def hybrid_layers(nc, x, wq, wk, wv, wo, w_gate, w_up, w_down, w_in, w_mg, w_out, cols, rows,
                  identity, head_mask, group_mask, key_pos, out):
    ctx = ExitStack()
    with ctx:
        def sb(name, shape, dt=F32, c=ctx):
            return c.enter_context(nc.sbuf_tensor(name, shape, dt))

        bank = [ctx.enter_context(nc.psum_tensor(f"bank{i}", [P, 512], F32)) for i in range(8)]

        X = sb("X", [P, TT, DM])
        ffnw = sb("ffnw", [P, FT, 3 * 512], BF16)
        wreg = sb("wreg", [P, 3 * KT * INNER])
        col = sb("col", [P, NCOL])
        row = sb("row", [P, 2, 512])
        ident = sb("ident", [P, P])
        hmask = sb("hmask", [P, P])
        gmask = sb("gmask", [P, HG])
        dtw = sb("dtw", [P, MT, P])
        negA = sb("negA", [P, MT])
        coef = sb("coef", [P, 8])
        ones32 = sb("ones32", [P, HD])
        ones_row = sb("ones_row", [3 * HG, SEQ], F32R)
        order_hl = sb("order_hl", [3 * HG, 2, SEQ], F32R)
        C_T, C_B, C_O, C_J, C_H, C_A, C_RA = range(7)

        att_w = wreg[:, 0:4 * KT * DM].rearrange("p (m k n) -> p m k n", m=4, k=KT)
        att_tail = wreg[:, 4 * KT * DM:]
        nT_att = att_tail[:, 0:KT * SEQ].rearrange("p (k n) -> p k n", k=KT)
        V = att_tail[:, KT * SEQ:].rearrange("p (t n) -> p t n", t=TT)
        mix_in = wreg[:, 0:KT * INNER].rearrange("p (k n) -> p k n", k=KT)
        mix_gate = wreg[:, KT * INNER:2 * KT * INNER].rearrange("p (k n) -> p k n", k=KT)
        mix_out = wreg[:, 2 * KT * INNER:].rearrange("p (j n) -> p j n", j=MT)

        def c(name, j=0):
            return col[:, COLS[name] + j:COLS[name] + j + 1]

        def load_att_weights(sp, done):
            for m, w in enumerate((wq, wk, wv, wo)):
                sp.dma_start(att_w[:, m], w.rearrange("(k p) n -> p k n", p=P)).then_inc(done, 16)

        def load_mix_weights(sp, done):
            for dst, w in ((mix_in, w_in), (mix_gate, w_mg), (mix_out, w_out)):
                sp.dma_start(dst, w.rearrange("(k p) n -> p k n", p=P)).then_inc(done, 16)

        def move(eng, dst, src, done):
            eng.dma_start(dst.bitcast(F32), src.bitcast(F32)).then_inc(done, 16)

        @contextmanager
        def phase(name, sems, buffers):
            with ExitStack() as stack:
                ph = {n: stack.enter_context(nc.semaphore(f"{name}_{n}")) for n in sems}
                ph.update({n: sb(f"{name}_{n}", shape, dt, stack) for n, (shape, dt) in buffers.items()})
                with nc.Block() as block:
                    yield ph, block
                for n in sems:
                    nc.sync.sem_clear(ph[n])
                nc.all_engine_barrier()

        LN_SEMS = ["ln_chain", "normed", "turned"]
        LN_BUFS = {"bn": ([P, TT, 6], F32), "mv": ([P, TT, 2], F32), "ln_v": ([P, TT], F32),
                   "ln_y": ([P, TT], F32), "ln_t": ([P, TT], F32), "N": ([P, TT, DM], F32)}

        def layernorm_vector(dve, ph, x_loaded=None):
            n = 0
            if x_loaded is not None:
                dve.wait_ge(x_loaded, 16 * TT)
            for t in range(TT):
                dve.bn_stats(ph["bn"][:, t, :], X[:, t, :]).then_inc(ph["ln_chain"], 1)
            n += TT
            dve.wait_ge(ph["ln_chain"], n)
            for t in range(TT):
                dve.bn_aggr(ph["mv"][:, t, :], ph["bn"][:, t, :]).then_inc(ph["ln_chain"], 1)
            n += TT
            dve.wait_ge(ph["ln_chain"], n)
            v, y, w = ph["ln_v"][:, :], ph["ln_y"][:, :], ph["ln_t"][:, :]
            dve.tensor_scalar(v, ph["mv"][:, :, 1], EPS, None, ALU.add).then_inc(ph["ln_chain"], 1)
            n += 1
            dve.wait_ge(ph["ln_chain"], n)
            dve.tensor_scalar(w.bitcast(I32), v.bitcast(I32), 1, None,
                              ALU.logical_shift_right).then_inc(ph["ln_chain"], 1)
            n += 1
            dve.wait_ge(ph["ln_chain"], n)
            dve.tensor_scalar(y.bitcast(I32), w.bitcast(I32), -1, 0x5f3759df,
                              ALU.mult, ALU.add).then_inc(ph["ln_chain"], 1)
            n += 1
            for _ in range(3):
                dve.wait_ge(ph["ln_chain"], n)
                dve.tensor_tensor(w, y, y, ALU.mult).then_inc(ph["ln_chain"], 1)
                dve.wait_ge(ph["ln_chain"], n + 1)
                dve.scalar_tensor_tensor(out=w, in0=w, scalar=-0.5, in1=v, op0=ALU.mult,
                                         op1=ALU.mult).then_inc(ph["ln_chain"], 1)
                dve.wait_ge(ph["ln_chain"], n + 2)
                dve.scalar_tensor_tensor(out=y, in0=w, scalar=1.5, in1=y, op0=ALU.add,
                                         op1=ALU.mult).then_inc(ph["ln_chain"], 1)
                n += 3
            dve.wait_ge(ph["ln_chain"], n)
            for t in range(TT):
                dve.tensor_scalar(ph["N"][:, t, :], X[:, t, :], ph["mv"][:, t, 0:1], y[:, t:t + 1],
                                  ALU.subtract, ALU.mult).then_inc(ph["normed"], 1)

        def layernorm_turn(pe, ph):
            for k in range(KT):
                for t in range(TT):
                    if k == 0:
                        pe.wait_ge(ph["normed"], t + 1)
                    last = pe.transpose(bank[k][:, t * P:(t + 1) * P], ph["N"][:, t, k * P:(k + 1) * P],
                                        ident[:, :])
                last.then_inc(ph["turned"], 1)

        def setup():
            sems = ["loaded", "staged0", "staged1", "weights", "chain", "ones", "gate_exp", "tile_done"]
            bufs = {"stage": ([P, 2, 3 * 512], F32), "body": ([P, 3 * 512], FP8), "above": ([P, 3 * 512], FP8),
                    "below": ([P, 3 * 512], FP8), "far": ([P, 3 * 512], F32), "sg": ([P, 5], F32),
                    "pos": ([3 * HG, SEQ], F32), "o32": ([3 * HG, SEQ], F32), "one": ([3 * HG, SEQ], F32)}
            with phase("setup", sems, bufs) as (ph, block):
                staged = (ph["staged0"], ph["staged1"])

                @block.sync
                def _(sp):
                    for dst, src in ((col, cols), (row, rows), (ident, identity), (hmask, head_mask),
                                     (gmask, group_mask), (ph["pos"], key_pos)):
                        sp.dma_start(dst[:], src).then_inc(ph["loaded"], 16)
                    for i in range(FT):
                        if i >= 2:
                            sp.wait_ge(ph["tile_done"], i - 1)
                        f = slice(i * P, (i + 1) * P)
                        st = ph["stage"][:, i % 2].rearrange("p (m k n) -> p m k n", m=3, k=KT)
                        for m, w in enumerate((w_gate, w_up)):
                            sp.dma_start(st[:, m], w.rearrange("(k p) n -> p k n", p=P)[:, :, f])\
                                .then_inc(staged[i % 2], 16)
                        sp.dma_start(ph["stage"][:, i % 2, 1024:1536], w_down[f, :]).then_inc(staged[i % 2], 16)
                    load_att_weights(sp, ph["weights"])
                    sp.wait_ge(ph["weights"], 16 * 4)

                @block.vector
                def _(dve):
                    n = 0

                    def chained(ins):
                        nonlocal n
                        n += 1
                        ins.then_inc(ph["chain"], 1)
                        dve.wait_ge(ph["chain"], n)

                    chained(dve.memset(ones32[:, :], 1.0))
                    chained(dve.memset(ph["one"][:, :], 1.0))
                    chained(dve.tensor_copy(ones_row[:, :], ph["one"][:, :]))
                    dve.wait_ge(ph["loaded"], 16 * 6)
                    for j in range(MT):
                        chained(dve.tensor_scalar(dtw[:, j, :], hmask[:, :], c("dt_w", j), None, ALU.mult))
                    dve.wait_ge(ph["gate_exp"], 1)
                    chained(dve.tensor_scalar(ph["sg"][:, :], ph["sg"][:, :], 1.0, None, ALU.add))
                    chained(dve.reciprocal(ph["sg"][:, :], ph["sg"][:, :]))
                    for k, (g, f) in {C_T: (0, -0.01), C_B: (1, 0.1 / math.log(SEQ)), C_O: (2, 1.0),
                                      C_J: (3, 0.1), C_H: (4, -0.1 / (SEQ - 1))}.items():
                        chained(dve.tensor_scalar(coef[:, k:k + 1], ph["sg"][:, g:g + 1], f, None, ALU.mult))
                    chained(dve.tensor_scalar(coef[:, C_A:C_A + 1], coef[:, C_J:C_J + 1], -1.0, 1.0,
                                              ALU.mult, ALU.add))
                    chained(dve.reciprocal(coef[:, C_RA:C_RA + 1], coef[:, C_A:C_A + 1]))
                    chained(dve.tensor_scalar(ph["o32"][:, :], ph["pos"][:, :], coef[0:3 * HG, C_O:C_O + 1],
                                              coef[0:3 * HG, C_RA:C_RA + 1], ALU.mult, ALU.mult))
                    chained(dve.tensor_copy(order_hl[:, 0, :], ph["o32"][:, :]))
                    chained(dve.tensor_tensor(order_hl[:, 1, :], ph["o32"][:, :],
                                              order_hl[:, 0, :].bitcast(F32), ALU.subtract))
                    dve.wait_ge(ph["gate_exp"], 2)
                    chained(dve.tensor_scalar(negA[:, :], negA[:, :], -1.0, None, ALU.mult))
                    for i in range(FT):
                        dve.wait_ge(staged[i % 2], 48 * (i // 2 + 1))
                        w = ph["stage"][:, i % 2, :]
                        dve.tensor_scalar(ph["body"][:, :], w, 128.0, -128.0, ALU.min, ALU.max,
                                          saturate=False).then_inc(ph["chain"], 1)
                        dve.tensor_scalar(ph["above"][:, :], w, 128.0, 0.5, ALU.max, ALU.mult,
                                          saturate=False).then_inc(ph["chain"], 1)
                        dve.tensor_scalar(ph["below"][:, :], w, -128.0, 0.5, ALU.min, ALU.mult,
                                          saturate=False).then_inc(ph["tile_done"], 1)
                        n += 2
                        dve.wait_ge(ph["chain"], n)
                        dve.wait_ge(ph["tile_done"], i + 1)
                        chained(dve.tensor_tensor(ph["far"][:, :], ph["above"][:, :], ph["below"][:, :], ALU.add))
                        chained(dve.scalar_tensor_tensor(out=ffnw[:, i, :], in0=ph["far"][:, :], scalar=2.0,
                                                         in1=ph["body"][:, :], op0=ALU.mult, op1=ALU.add))

                @block.scalar
                def _(act):
                    act.wait_ge(ph["loaded"], 16 * 6)
                    g = COLS["gates"]
                    act.activation(ph["sg"][:, :], col[:, g:g + 5], ACT.Exp, scale=-1.0).then_inc(ph["gate_exp"], 1)
                    a = COLS["A_log"]
                    act.activation(negA[:, :], col[:, a:a + MT], ACT.Exp).then_inc(ph["gate_exp"], 1)

        def attention(b):
            order = ["q0", "k0"] + [f"v{t}" for t in range(TT)] + ["s0"]
            for g in range(GROUPS):
                if g < GROUPS - 1:
                    order += [f"q{g + 1}", f"k{g + 1}", f"s{g + 1}"]
                order += [f"r{g}"]
            order += [f"o{t}" for t in range(TT)]
            PROJ, PROB = 4, 5
            place = {"v0": 0, "v1": 1, "v2": 2, "v3": 3, "q0": 4, "k0": 6, "s0": 7,
                     "o0": 0, "o1": 1, "o2": 2, "o3": 3}

            def at(name):
                return bank[place.get(name, PROB if name[0] == "r" else PROJ)]

            def score_bank(n):
                return bank[n % 3]

            sems = LN_SEMS + ["x_in", "nt_act", "nt_dve", "filled", "v_act", "v_dve",
                              "q_ready", "k_ready", "k2_ready", "dk_ready", "mean_w", "high", "low",
                              "const_rows", "stk0", "stk1", "score", "maxed", "exped", "ent", "diff", "diff_act",
                              "diff_dve", "prob_mm", "prob", "pv", "heads_out", "chain", "stat_read", "lns", "rz_ready", "shift", "shift_h",
                              "shift_l", "shift_rows", "xb", "x_out"]
            bufs = dict(LN_BUFS)
            bufs |= {"k32": ([P, SEQ], F32), "tmp": ([P, 6, SEQ], F32R), "Qs": ([P, 3, HG, SEQ], F32R),
                     "Ks": ([P, 3, HG, SEQ], F32R), "Ds": ([KSTK, 2, HG, SEQ], F32R), "E": ([P, 2, SEQ], F32),
                     "PT": ([P, 2, SEQ], F32), "rz": ([P, SEQ], F32),
                     "nmax": ([P, NS], F32), "Z": ([P, NS], F32), "U": ([P, NS], F32), "Ab": ([P, NS], F32),
                     "stat": ([P, GROUPS, 2, TT, HG], F32), "ksum": ([P, GROUPS], F32),
                     "meanw": ([P, GROUPS, HG], F32), "w": ([P, 6, GT], F32), "r": ([P, GT], F32),
                     "rh": ([GT, P], F32R), "rl": ([GT, P], F32R)}
            with phase("att", sems, bufs) as (ph, block):
                OT = ph["N"]
                q32, dk, k2 = ph["N"][:, 1, :], ph["N"][:, 2, :], ph["N"][:, 3, :]
                QH, QL, KH, KL, DH, DL = range(6)

                def stacked(eng, g):
                    eng.wait_ge((ph["stk0"], ph["stk1"])[g % 2], 16 * 9 * (g // 2 + 1))

                def filled(eng, name):
                    eng.wait_ge(ph["filled"], order.index(name) + 1)

                @block.sync
                def _(sp):
                    for t in range(TT):
                        sp.dma_start(X[:, t, :], x[b, t * P:(t + 1) * P, :]).then_inc(ph["x_in"], 16)
                    def const_rows():
                        for dst, row0, src in (("Ks", ROW_R, ones_row[:, :]), ("Ks", ROW_R + 1, ones_row[:, :]),
                                               ("Ks", ROW_O, order_hl[:, 0, :]), ("Ks", ROW_O + 1, order_hl[:, 1, :]),
                                               ("Qs", ROW_O, ones_row[:, :]), ("Qs", ROW_O + 1, ones_row[:, :])):
                            move(sp, ph[dst][row0:row0 + 1], src, ph["const_rows"])

                    def stack_up(g):
                        if g >= 2:
                            sp.wait_ge(ph["diff"], GT * (g - 1))
                        if g >= 3:
                            sp.wait_ge(ph["prob_mm"], GT * (g - 2))
                        sp.wait_ge(ph["high"], 3 * (g + 1))
                        sp.wait_ge(ph["low"], 3 * (g + 1))
                        for dst, parts in ((ph["Qs"][:, g % 3], (QH, QH, QL)), (ph["Ks"][:, g % 3], (KH, KL, KH)),
                                           (ph["Ds"][:, g % 2], (DH, DL, DH))):
                            for i, part in enumerate(parts):
                                move(sp, dst[HD * i:HD * (i + 1)],
                                     ph["tmp"][:, part, :],
                                     (ph["stk0"], ph["stk1"])[g % 2])

                    def shift_rows(g):
                        sp.wait_ge(ph["shift_h"], g + 1)
                        sp.wait_ge(ph["shift_l"], g + 1)
                        move(sp, ph["Qs"][ROW_R:ROW_R + 1, g % 3], ph["rh"][:, :], ph["shift_rows"])
                        move(sp, ph["Qs"][ROW_R + 1:ROW_R + 2, g % 3], ph["rl"][:, :], ph["shift_rows"])

                    stack_up(0)
                    const_rows()
                    for g in range(GROUPS):
                        if g + 1 < GROUPS:
                            stack_up(g + 1)
                        shift_rows(g)
                    sp.wait_ge(ph["shift_rows"], 32 * GROUPS)

                @block.tensor
                def _(pe):
                    layernorm_turn(pe, ph)
                    pe.wait_ge(ph["nt_act"], 2)
                    pe.wait_ge(ph["nt_dve"], 2)
                    def project(g, name, m, ks=range(KT)):
                        for k in ks:
                            last = pe.matmul(at(f"{name}{g}")[:, :], att_w[:, m, k, g * P:(g + 1) * P],
                                             nT_att[:, k, :], start=(k == 0), stop=(k == KT - 1))
                        if k == KT - 1:
                            last.then_inc(ph["filled"], 1)

                    def key_stats(g):
                        pe.wait_ge(ph["k2_ready"], g + 1)
                        pe.wait_ge(ph["q_ready"], g + 1)
                        pe.wait_ge(ph["mean_w"], g + 1)
                        to = at(f"s{g}")
                        for t in range(TT):
                            pe.matmul(to[:, HG * t:HG * (t + 1)], k2[:, t * P:(t + 1) * P], gmask[:, :],
                                      start=True, stop=True)
                            last = pe.matmul(to[:, GT + HG * t:GT + HG * (t + 1)], q32[:, t * P:(t + 1) * P],
                                             ph["meanw"][:, g, :], start=True, stop=True)
                        last.then_inc(ph["filled"], 1)

                    project(0, "q", 0)
                    project(0, "k", 1)
                    for t in range(TT):
                        for k in range(KT):
                            last = pe.matmul(at(f"v{t}")[:, :], nT_att[:, k, t * P:(t + 1) * P],
                                             att_w[:, 2, k, :], start=(k == 0), stop=(k == KT - 1))
                        last.then_inc(ph["filled"], 1)
                    key_stats(0)
                    for n in range(NS + LAG + 1):
                        g, i = divmod(n, GT)
                        if n < NS:
                            h, t = divmod(i, TT)
                            if i == 0:
                                stacked(pe, g)
                            if n == 0:
                                pe.wait_ge(ph["v_act"], 2)
                                pe.wait_ge(ph["v_dve"], 2)
                            if n >= 3:
                                pe.wait_ge(ph["ent"], n - 2)
                            pe.matmul(score_bank(n)[:, :], ph["Qs"][0:KSTK, g % 3, h, t * P:(t + 1) * P],
                                      ph["Ks"][0:KSTK, g % 3, h, :], start=True, stop=True).then_inc(ph["score"], 1)
                        m = n - LAG
                        if 0 <= m < NS:
                            gm, im = divmod(m, GT)
                            h, k = divmod(im, TT)
                            if m == 0:
                                pe.wait_ge(ph["const_rows"], 16 * 6)
                            if im == 0:
                                pe.wait_ge(ph["shift_rows"], 32 * (gm + 1))
                            if im == (3 - LAG) % GT + 1 and gm < GROUPS - 1:
                                pe.wait_ge(ph["shift_l"], gm + 2)
                            elif m >= 1:
                                pe.wait_ge(ph["prob"], m)
                            pe.matmul(bank[PROB][:, :], ph["Ks"][0:KALL, gm % 3, h, k * P:(k + 1) * P],
                                      ph["Qs"][0:KALL, gm % 3, h, :], start=True, stop=True).then_inc(ph["prob_mm"], 1)
                        m -= 1
                        if 0 <= m < NS:
                            gm, im = divmod(m, GT)
                            h, k = divmod(im, TT)
                            pe.wait_ge(ph["prob"], m + 1)
                            if im == 0 and gm >= 1:
                                pe.wait_ge(ph["heads_out"], gm)
                            hs = slice(HD * h, HD * (h + 1))
                            vs = slice((gm * HG + h) * HD, (gm * HG + h + 1) * HD)
                            pe.matmul(bank[6][hs, :], V[:, k, vs], ph["PT"][:, m % 2, :], start=(k == 0),
                                      stop=(k == TT - 1), tile_position=(0, HD * h))
                            pe.matmul(bank[7][hs, :], ones32[:, :], ph["PT"][:, m % 2, :], start=(k == 0),
                                      stop=(k == TT - 1), tile_position=(0, HD * h)).then_inc(ph["pv"], 1)
                        if n < NS:
                            h, t = divmod(i, TT)
                            if n >= 1:
                                pe.wait_ge(ph["diff_act"] if n % 2 else ph["diff_dve"], (n + 1) // 2)
                            pe.matmul(bank[3][:, :], ph["Qs"][0:KSTK, g % 3, h, t * P:(t + 1) * P],
                                      ph["Ds"][:, g % 2, h, :], start=True, stop=True).then_inc(ph["diff"], 1)
                        if n >= GT and i == 3 and g <= GROUPS:
                            gr = g - 1
                            pe.wait_ge(ph["shift"], gr + 1)
                            if n > LAG:
                                pe.wait_ge(ph["prob"], n - LAG + 1)
                            pe.transpose(at(f"r{gr}")[0:GT, 0:P], ph["r"][:, :], ident[:, :])\
                                .then_inc(ph["filled"], 1)
                        if g + 1 < GROUPS:
                            if i == 4:
                                pe.wait_ge(ph["stat_read"], g + 1)
                            if i in (4, 5):
                                project(g + 1, "q", 0, range(2 * (i - 4), 2 * (i - 3)))
                            if i == 6:
                                pe.wait_ge(ph["q_ready"], g + 2)
                            if i in (6, 7):
                                project(g + 1, "k", 1, range(2 * (i - 6), 2 * (i - 5)))
                            if i == 11:
                                key_stats(g + 1)
                    pe.wait_ge(ph["heads_out"], GROUPS)
                    pe.wait_ge(ph["ent"], NS)
                    pe.wait_ge(ph["diff_dve"], NS // 2)
                    pe.wait_ge(ph["diff_act"], NS // 2)
                    for t in range(TT):
                        for g in range(GROUPS):
                            last = pe.matmul(at(f"o{t}")[:, :], OT[:, g, t * P:(t + 1) * P],
                                             att_w[:, 3, g, :], start=(g == 0), stop=(g == GROUPS - 1))
                        last.then_inc(ph["filled"], 1)

                @block.scalar
                def _(act):
                    act.preload_act_table_set("natural_log_exp_and_others")
                    for k in (0, 2):
                        act.wait_ge(ph["turned"], k + 1)
                        act.activation(nT_att[:, k, :], bank[k][:, :], ACT.Copy).then_inc(ph["nt_act"], 1)
                    def key(g):
                        filled(act, f"k{g}")
                        if g >= 1:
                            act.wait_ge(ph["low"], 3 * g)
                            act.wait_ge(ph["k2_ready"], g)
                        act.activation(ph["k32"][:, :], at(f"k{g}")[:, :], ACT.Identity, bias=c("bk", g),
                                       accum_out=ph["ksum"][:, g:g + 1]).then_inc(ph["k_ready"], 1)

                    key(0)
                    for t in (0, 2):
                        filled(act, f"v{t}")
                        act.activation(V[:, t, :], at(f"v{t}")[:, :], ACT.Copy)\
                            .then_inc(ph["v_act"], 1)
                    for n in range(NS + LAG):
                        g, i = divmod(n, GT)
                        if g + 1 < GROUPS and i == 8:
                            key(g + 1)
                        if n >= GT and i == 4 and g <= GROUPS:
                            gr = g - 1
                            filled(act, f"r{gr}")
                            if gr >= 1:
                                act.wait_ge(ph["shift_rows"], 32 * gr)
                            act.activation(ph["rh"][:, :], at(f"r{gr}")[0:GT, 0:P], ACT.Copy)\
                                .then_inc(ph["shift_h"], 1)
                        if n < NS:
                            act.wait_ge(ph["maxed"], n + 1)
                            if n >= 2:
                                act.wait_ge(ph["ent"], n - 1)
                            act.activation(ph["E"][:, n % 2, :], score_bank(n)[:, :], ACT.Exp,
                                           bias=ph["nmax"][:, n:n + 1], accum_out=ph["Z"][:, n:n + 1])\
                                .then_inc(ph["exped"], 1)
                            if n % 2 == 0:
                                act.wait_ge(ph["diff"], n + 1)
                                act.activation(bank[3][:, :], bank[3][:, :], ACT.Abs,
                                               accum_out=ph["Ab"][:, n:n + 1]).then_inc(ph["diff_act"], 1)
                        if n >= GT and i == 1 and g <= GROUPS:
                            gr = g - 1
                            s = slice(gr * GT, (gr + 1) * GT)
                            act.wait_ge(ph["exped"], GT * (gr + 1))
                            act.activation(ph["w"][:, 0, :], ph["Z"][:, s], ACT.Ln).then_inc(ph["lns"], 1)
                            kn = ph["w"][:, 1, :].rearrange("p (h t) -> p t h", h=HG)
                            act.activation(kn, ph["stat"][:, gr, 0], ACT.Ln).then_inc(ph["lns"], 1)
                            act.wait_ge(ph["lns"], 3 * gr + 2)
                            act.activation(ph["w"][:, 2, :], ph["w"][:, 1, :], ACT.Exp, scale=0.5).then_inc(ph["lns"], 1)
                        m = n - LAG
                        if m >= 0:
                            act.wait_ge(ph["prob_mm"], m + 1)
                            if m >= 2:
                                act.wait_ge(ph["pv"], m - 1)
                            act.activation(ph["PT"][:, m % 2, :], bank[PROB][:, :], ACT.Exp,
                                           scale=coef[:, C_A:C_A + 1]).then_inc(ph["prob"], 1)
                            if m % GT == GT - 1:
                                act.wait_ge(ph["pv"], m + 1)
                                if m >= GT:
                                    act.wait_ge(ph["heads_out"], m // GT)
                                act.activation(ph["rz"][:, :], bank[7][:, :], ACT.Ln).then_inc(ph["rz_ready"], 1)
                                act.wait_ge(ph["rz_ready"], 2 * (m // GT) + 1)
                                act.activation(ph["rz"][:, :], ph["rz"][:, :], ACT.Exp, scale=-1.0)\
                                    .then_inc(ph["rz_ready"], 1)

                @block.vector
                def _(dve):
                    layernorm_vector(dve, ph, ph["x_in"])
                    for k in (1, 3):
                        dve.wait_ge(ph["turned"], k + 1)
                        dve.tensor_copy(nT_att[:, k, :], bank[k][:, :]).then_inc(ph["nt_dve"], 1)
                    def query(g):
                        filled(dve, f"q{g}")
                        if g >= 1:
                            dve.wait_ge(ph["low"], 3 * g)
                        else:
                            dve.wait_ge(ph["turned"], KT)
                        dve.tensor_scalar(q32, at(f"q{g}")[:, :], c("bq", g), 1 / math.sqrt(HD),
                                          ALU.add, ALU.mult).then_inc(ph["q_ready"], 1)
                        dve.wait_ge(ph["q_ready"], g + 1)
                        if g >= 1:
                            stacked(dve, g - 1)
                        dve.tensor_copy(ph["tmp"][:, QH, :], q32).then_inc(ph["high"], 1)

                    def key(g):
                        dve.wait_ge(ph["k_ready"], g + 1)
                        dve.tensor_scalar(ph["meanw"][:, g, :], gmask[:, :], ph["ksum"][:, g:g + 1], 1 / SEQ,
                                          ALU.mult, ALU.mult).then_inc(ph["mean_w"], 1)
                        dve.tensor_copy(ph["tmp"][:, KH, :], ph["k32"][:, :]).then_inc(ph["high"], 1)
                        dve.wait_ge(ph["dk_ready"], g + 1)
                        dve.tensor_copy(ph["tmp"][:, DH, :], dk).then_inc(ph["high"], 1)

                    def stats(g):
                        filled(dve, f"s{g}")
                        src = at(f"s{g}")[:, 0:2 * GT].rearrange("p (m t h) -> p m t h", m=2, t=TT)
                        dve.tensor_scalar(ph["stat"][:, g, 0], src[:, 0], 1e-18, None, ALU.max)\
                            .then_inc(ph["chain"], 1)
                        dve.tensor_copy(ph["stat"][:, g, 1], src[:, 1]).then_inc(ph["stat_read"], 1)

                    query(0)
                    key(0)
                    for t in (1, 3):
                        filled(dve, f"v{t}")
                        dve.tensor_copy(V[:, t, :], at(f"v{t}")[:, :])\
                            .then_inc(ph["v_dve"], 1)
                    stats(0)
                    chain = 1
                    for n in range(NS + LAG + 2):
                        g, i = divmod(n, GT)
                        if g + 1 < GROUPS:
                            if i == 6:
                                query(g + 1)
                            if i == 9:
                                key(g + 1)
                            if i == 12:
                                stats(g + 1)
                                chain += 1
                        if 1 <= n <= NS:
                            m = n - 1
                            if m % 2 == 1:
                                dve.wait_ge(ph["diff"], m + 1)
                                dve.tensor_reduce(ph["Ab"][:, m:m + 1], bank[3][:, :], AX, ALU.add,
                                                  apply_absolute_value=True).then_inc(ph["diff_dve"], 1)
                        if n < NS:
                            dve.wait_ge(ph["score"], n + 1)
                            dve.tensor_reduce(ph["nmax"][:, n:n + 1], score_bank(n)[:, :], AX, ALU.max, negate=True)\
                                .then_inc(ph["maxed"], 1)
                        if 1 <= n <= NS:
                            m = n - 1
                            dve.wait_ge(ph["exped"], m + 1)
                            dve.scalar_tensor_tensor(out=ph["E"][:, m % 2, :], in0=score_bank(m)[:, :],
                                                     scalar=ph["nmax"][:, m:m + 1], in1=ph["E"][:, m % 2, :],
                                                     op0=ALU.add, op1=ALU.mult, accum_out=ph["U"][:, m:m + 1])\
                                .then_inc(ph["ent"], 1)
                        if n >= GT and i == 1 and g <= GROUPS:
                            gr = g - 1
                            s = slice(gr * GT, (gr + 1) * GT)
                            w = ph["w"]

                            def chained(ins):
                                nonlocal chain
                                chain += 1
                                ins.then_inc(ph["chain"], 1)
                                dve.wait_ge(ph["chain"], chain)

                            def k_(j):
                                return coef[:, j:j + 1]

                            dve.wait_ge(ph["ent"], GT * (gr + 1))
                            dve.wait_ge(ph["lns"], 3 * (gr + 1))
                            dve.wait_ge(ph["diff_act"], GT // 2 * (gr + 1))
                            dve.wait_ge(ph["diff_dve"], GT // 2 * (gr + 1))
                            mean = ph["stat"][:, gr, 1].rearrange("p t h -> p h t")
                            acc = w[:, 4, :]
                            acc_ht = acc.rearrange("p (h t) -> p h t", h=HG)
                            chained(dve.reciprocal(w[:, 3, :], ph["Z"][:, s]))
                            chained(dve.tensor_tensor(w[:, 3, :], w[:, 3, :], ph["U"][:, s], ALU.mult))
                            chained(dve.tensor_tensor(w[:, 3, :], w[:, 0, :], w[:, 3, :], ALU.subtract))
                            chained(dve.tensor_scalar(acc, w[:, 2, :], k_(C_T), None, ALU.mult))
                            chained(dve.scalar_tensor_tensor(out=acc, in0=w[:, 3, :], scalar=k_(C_B), in1=acc,
                                                             op0=ALU.mult, op1=ALU.add))
                            chained(dve.scalar_tensor_tensor(out=acc_ht, in0=mean, scalar=k_(C_J), in1=acc_ht,
                                                             op0=ALU.mult, op1=ALU.add))
                            chained(dve.scalar_tensor_tensor(out=acc, in0=ph["Ab"][:, s], scalar=k_(C_H), in1=acc,
                                                             op0=ALU.mult, op1=ALU.add))
                            chained(dve.scalar_tensor_tensor(out=w[:, 5, :], in0=ph["nmax"][:, s], scalar=k_(C_A),
                                                             in1=acc, op0=ALU.mult, op1=ALU.subtract))
                            chained(dve.tensor_tensor(acc, w[:, 5, :], acc, ALU.add))
                            if gr >= 1:
                                dve.wait_ge(ph["shift_h"], gr)
                            dve.tensor_scalar(ph["r"][:, :], acc, k_(C_RA), None, ALU.mult).then_inc(ph["shift"], 1)
                        if n >= GT and i == 4 and g <= GROUPS:
                            gr = g - 1
                            dve.wait_ge(ph["shift_h"], gr + 1)
                            if gr >= 1:
                                dve.wait_ge(ph["shift_rows"], 32 * gr)
                            dve.tensor_tensor(ph["rl"][:, :], at(f"r{gr}")[0:GT, 0:P],
                                              ph["rh"][:, :].bitcast(F32), ALU.subtract).then_inc(ph["shift_l"], 1)
                        m = n - LAG - 1
                        if m >= 0 and m % GT == GT - 1:
                            gm = m // GT
                            dve.wait_ge(ph["pv"], m + 1)
                            dve.wait_ge(ph["rz_ready"], 2 * (gm + 1))
                            heads = OT[:, gm, :]
                            dve.tensor_tensor(heads, bank[7][:, :], ph["rz"][:, :], ALU.mult)\
                                .then_inc(ph["chain"], 1)
                            dve.wait_ge(ph["chain"], chain + 1)
                            dve.scalar_tensor_tensor(out=heads, in0=heads, scalar=-2.0,
                                                     in1=ph["rz"][:, :], op0=ALU.add, op1=ALU.mult)\
                                .then_inc(ph["chain"], 1)
                            dve.wait_ge(ph["chain"], chain + 2)
                            dve.scalar_tensor_tensor(out=heads, in0=bank[6][:, :], scalar=-1.0,
                                                     in1=heads, op0=ALU.mult, op1=ALU.mult)\
                                .then_inc(ph["chain"], 1)
                            chain += 3
                            dve.wait_ge(ph["chain"], chain)
                            dve.tensor_scalar(heads, heads, c("bv", gm), None, ALU.add)\
                                .then_inc(ph["heads_out"], 1)
                    for t in range(TT):
                        filled(dve, f"o{t}")
                        dve.wait_ge(ph["xb"], t + 1)
                        dve.tensor_tensor(X[:, t, :], at(f"o{t}")[:, :], X[:, t, :], ALU.add)\
                            .then_inc(ph["x_out"], 1)

                @block.gpsimd
                def _(pool):
                    for g in range(GROUPS):
                        pool.wait_ge(ph["k_ready"], g + 1)
                        pool.wait_ge(ph["turned"], KT)
                        if g >= 1:
                            pool.wait_ge(ph["filled"], order.index(f"s{g - 1}") + 1)
                            pool.wait_ge(ph["high"], 3 * g)
                        pool.tensor_tensor(k2, ph["k32"][:, :], ph["k32"][:, :], ALU.mult).then_inc(ph["k2_ready"], 1)
                        if g == 0:
                            pool.memset(dk[:, SEQ - 1:SEQ], 0.0)
                        pool.tensor_tensor(dk[:, 0:SEQ - 1], ph["k32"][:, 1:SEQ], ph["k32"][:, 0:SEQ - 1],
                                           ALU.subtract).then_inc(ph["dk_ready"], 1)
                        pool.wait_ge(ph["dk_ready"], g + 1)
                        if g >= 1:
                            stacked(pool, g - 1)
                        for i, (full, hi, lo) in enumerate(((q32, QH, QL), (ph["k32"][:, :], KH, KL), (dk, DH, DL))):
                            pool.wait_ge(ph["high"], 3 * g + i + 1)
                            pool.tensor_tensor(ph["tmp"][:, lo, :], full, ph["tmp"][:, hi, :].bitcast(F32),
                                               ALU.subtract).then_inc(ph["low"], 1)
                    for t in range(TT):
                        pool.wait_ge(ph["normed"], t + 1)
                        pool.tensor_tensor(X[:, t, :], X[:, t, :], row[:, 0, :], ALU.add).then_inc(ph["xb"], 1)

        def ffn(name, load_next, store_to=None):
            sems = LN_SEMS + ["n_high", "n_low", "w32", "gate_mm", "up_mm", "silu", "hid", "h_high", "h_low",
                              "down", "scaled", "x_out", "next_w", "stored"]
            bufs = dict(LN_BUFS)
            bufs |= {"nH": ([P, KT, SEQ], F32R), "nL": ([P, KT, SEQ], F32R), "wf": ([P, 3, 3, 512], F32R),
                     "sg": ([P, 2, SEQ], F32), "h32": ([P, 2, SEQ], F32), "hH": ([P, 3, SEQ], F32R),
                     "hL": ([P, 3, SEQ], F32R), "y": ([P, 2, 512], F32)}
            with phase(name, sems, bufs) as (ph, block):
                @block.sync
                def _(sp):
                    load_next(sp, ph["next_w"])
                    if store_to is not None:
                        for t in range(TT):
                            sp.wait_ge(ph["x_out"], t + 1)
                            sp.dma_start(out[store_to, t * P:(t + 1) * P, :], X[:, t, :]).then_inc(ph["stored"], 16)
                        sp.wait_ge(ph["stored"], 16 * TT)
                        sp.wait_ge(ph["next_w"], 16 * 4)
                    else:
                        sp.wait_ge(ph["next_w"], 16 * 3)

                @block.tensor
                def _(pe):
                    layernorm_turn(pe, ph)
                    pe.wait_ge(ph["n_low"], KT)
                    def up(i):
                        for j, (done, used) in enumerate(((ph["gate_mm"], ph["silu"]), (ph["up_mm"], ph["hid"]))):
                            if i >= 2:
                                pe.wait_ge(used, i - 1)
                            w = ph["wf"][:, i % 3, j, :].rearrange("p (k n) -> p k n", k=KT)
                            for k in range(KT):
                                for part in (ph["nH"], ph["nL"]):
                                    last = pe.matmul(bank[2 * j + i % 2][:, :], w[:, k, :], part[:, k, :],
                                                     start=(k == 0 and part is ph["nH"]),
                                                     stop=(k == KT - 1 and part is ph["nL"]))
                            last.then_inc(done, 1)

                    def down(i):
                        pe.wait_ge(ph["h_low"], i + 1)
                        for t in range(TT):
                            for part in (ph["hH"], ph["hL"]):
                                last = pe.matmul(bank[4 + t][:, :], part[:, i % 3, t * P:(t + 1) * P],
                                                 ph["wf"][:, i % 3, 2, :], start=(i == 0 and part is ph["hH"]),
                                                 stop=(i == FT - 1 and part is ph["hL"]))
                        last.then_inc(ph["down"], 1)

                    for i in range(FT):
                        pe.wait_ge(ph["w32"], i + 1)
                        up(i)
                        if i >= 1:
                            down(i - 1)
                    down(FT - 1)

                @block.scalar
                def _(act):
                    def widen(i):
                        if i >= 3:
                            act.wait_ge(ph["down"], i - 2)
                        act.activation(ph["wf"][:, i % 3].rearrange("p m n -> p (m n)"), ffnw[:, i, :], ACT.Copy)\
                            .then_inc(ph["w32"], 1)

                    widen(0)
                    widen(1)
                    for k in range(KT):
                        act.wait_ge(ph["turned"], k + 1)
                        act.activation(ph["nH"][:, k, :], bank[k][:, :], ACT.Copy).then_inc(ph["n_high"], 1)
                    for i in range(FT):
                        act.wait_ge(ph["gate_mm"], i + 1)
                        if i >= 2:
                            act.wait_ge(ph["hid"], i - 1)
                        act.activation(ph["sg"][:, i % 2, :], bank[i % 2][:, :], ACT.Silu,
                                       scale=c("gate_scale", i)).then_inc(ph["silu"], 1)
                        if i + 2 < FT:
                            widen(i + 2)

                @block.vector
                def _(dve):
                    layernorm_vector(dve, ph)
                    for k in range(KT):
                        dve.wait_ge(ph["n_high"], k + 1)
                        dve.tensor_tensor(ph["nL"][:, k, :], bank[k][:, :], ph["nH"][:, k, :].bitcast(F32),
                                          ALU.subtract).then_inc(ph["n_low"], 1)
                    for i in range(FT):
                        dve.wait_ge(ph["up_mm"], i + 1)
                        dve.wait_ge(ph["silu"], i + 1)
                        dve.scalar_tensor_tensor(out=ph["h32"][:, i % 2, :], in0=bank[2 + i % 2][:, :],
                                                 scalar=c("up_scale", i), in1=ph["sg"][:, i % 2, :],
                                                 op0=ALU.mult, op1=ALU.mult).then_inc(ph["hid"], 1)
                        dve.wait_ge(ph["hid"], i + 1)
                        if i >= 3:
                            dve.wait_ge(ph["down"], i - 2)
                        dve.tensor_copy(ph["hH"][:, i % 3, :], ph["h32"][:, i % 2, :]).then_inc(ph["h_high"], 1)
                        dve.wait_ge(ph["h_high"], i + 1)
                        dve.tensor_tensor(ph["hL"][:, i % 3, :], ph["h32"][:, i % 2, :],
                                          ph["hH"][:, i % 3, :].bitcast(F32), ALU.subtract).then_inc(ph["h_low"], 1)
                    dve.wait_ge(ph["down"], FT)
                    for t in range(TT):
                        if t >= 2:
                            dve.wait_ge(ph["x_out"], t - 1)
                        dve.tensor_tensor(ph["y"][:, t % 2, :], bank[4 + t][:, :], row[:, 1, :], ALU.mult)\
                            .then_inc(ph["scaled"], 1)
                        dve.wait_ge(ph["scaled"], t + 1)
                        dve.tensor_tensor(X[:, t, :], X[:, t, :], ph["y"][:, t % 2, :], ALU.add)\
                            .then_inc(ph["x_out"], 1)

        def mixer():
            sems = LN_SEMS + ["nt_act", "nt_dve", "in_mm", "gate_mm", "pads", "proj", "conv", "convd", "sig", "act_x",
                              "gated", "dt_mm", "e_chain", "relu", "dt", "decay", "drive", "scan", "skip", "y",
                              "comb", "out_mm", "x_out"]
            bufs = dict(LN_BUFS)
            bufs |= {"nT": ([P, KT, SEQ], F32), "pj": ([P, 2, SEQ + DCONV - 1], F32), "cv": ([P, 2, SEQ], F32),
                     "sg": ([P, 2, SEQ], F32), "Xs": ([P, MT, SEQ], F32), "gate": ([P, MT, SEQ], F32),
                     "ea": ([P, 2, SEQ], F32), "el": ([P, 2, SEQ], F32), "rl": ([P, 2, SEQ], F32),
                     "dtv": ([P, 2, SEQ], F32), "dec": ([P, 2, SEQ], F32), "drv": ([P, 2, SEQ], F32),
                     "st": ([P, 2, SEQ], F32), "sk": ([P, 2, SEQ], F32), "cb": ([P, 2, SEQ], F32)}
            with phase("mix", sems, bufs) as (ph, block):
                @block.tensor
                def _(pe):
                    layernorm_turn(pe, ph)
                    pe.wait_ge(ph["nt_act"], 2)
                    pe.wait_ge(ph["nt_dve"], 2)
                    for j in range(MT):
                        for o, (w, done, used) in enumerate(((mix_in, ph["in_mm"], ph["proj"]),
                                                             (mix_gate, ph["gate_mm"], ph["gated"]))):
                            if j >= 2:
                                pe.wait_ge(used, j - 1)
                            for k in range(KT):
                                last = pe.matmul(bank[2 * o + j % 2][:, :], w[:, k, j * P:(j + 1) * P],
                                                 ph["nT"][:, k, :], start=(k == 0), stop=(k == KT - 1))
                            last.then_inc(done, 1)

                    def project_out(j):
                        pe.wait_ge(ph["comb"], j + 1)
                        for t in range(TT):
                            last = pe.matmul(bank[4 + t][:, :], ph["cb"][:, j % 2, t * P:(t + 1) * P],
                                             mix_out[:, j, :], start=(j == 0), stop=(j == MT - 1))
                        last.then_inc(ph["out_mm"], 1)

                    for j in range(MT):
                        pe.wait_ge(ph["act_x"], j + 1)
                        if j < 2:
                            pe.wait_ge(ph["proj"], MT)
                        else:
                            pe.wait_ge(ph["relu"], j - 1)
                        pe.matmul(bank[j % 2][:, :], dtw[:, j, :], ph["Xs"][:, j, :], start=True, stop=True)\
                            .then_inc(ph["dt_mm"], 1)
                        if j >= 1:
                            project_out(j - 1)
                    project_out(MT - 1)

                @block.scalar
                def _(act):
                    for k in (0, 2):
                        act.wait_ge(ph["turned"], k + 1)
                        act.activation(ph["nT"][:, k, :], bank[k][:, :], ACT.Copy).then_inc(ph["nt_act"], 1)

                    def silu_gate(j):
                        act.wait_ge(ph["convd"], j + 1)
                        if j >= 2:
                            act.wait_ge(ph["act_x"], j - 1)
                        act.activation(ph["sg"][:, j % 2, :], ph["cv"][:, j % 2, :], ACT.Sigmoid).then_inc(ph["sig"], 1)

                    for j in range(MT):
                        act.wait_ge(ph["in_mm"], j + 1)
                        act.wait_ge(ph["pads"], 2)
                        if j >= 2:
                            act.wait_ge(ph["convd"], j - 1)
                        act.activation(ph["pj"][:, j % 2, DCONV - 1:], bank[j % 2][:, :], ACT.Copy)\
                            .then_inc(ph["proj"], 1)
                        act.wait_ge(ph["gate_mm"], j + 1)
                        act.activation(ph["gate"][:, j, :], bank[2 + j % 2][:, :], ACT.Sigmoid)\
                            .then_inc(ph["gated"], 1)
                        if j >= 1:
                            silu_gate(j - 1)
                    silu_gate(MT - 1)
                    act.preload_act_table_set("natural_log_exp_and_others")
                    for j in range(MT):
                        s = j % 2
                        act.wait_ge(ph["dt_mm"], j + 1)
                        act.activation(ph["ea"][:, s, :], bank[s][:, :], ACT.Abs, bias=c("dt_b", j))\
                            .then_inc(ph["e_chain"], 1)
                        act.wait_ge(ph["e_chain"], 2 * j + 1)
                        act.activation(ph["ea"][:, s, :], ph["ea"][:, s, :], ACT.Exp, scale=-1.0).then_inc(ph["e_chain"], 1)
                        act.wait_ge(ph["e_chain"], 2 * j + 2)
                        if j >= 2:
                            act.wait_ge(ph["dt"], j - 1)
                        act.activation(ph["el"][:, s, :], ph["ea"][:, s, :], ACT.Ln, bias=1.0).then_inc(ph["conv"], 1)
                        act.wait_ge(ph["dt"], j + 1)
                        if j >= 2:
                            act.wait_ge(ph["scan"], j - 1)
                        act.activation(ph["dec"][:, s, :], ph["dtv"][:, s, :], ACT.Exp, scale=negA[:, j:j + 1])\
                            .then_inc(ph["decay"], 1)

                @block.vector
                def _(dve):
                    layernorm_vector(dve, ph)
                    for k in (1, 3):
                        dve.wait_ge(ph["turned"], k + 1)
                        dve.tensor_copy(ph["nT"][:, k, :], bank[k][:, :]).then_inc(ph["nt_dve"], 1)
                    n = 0
                    for j in range(MT):
                        s = j % 2
                        dve.wait_ge(ph["proj"], j + 1)
                        if j >= 2:
                            dve.wait_ge(ph["act_x"], j - 1)
                        cv = ph["cv"][:, s, :]
                        w = COLS["conv_w"] + j * DCONV
                        dve.tensor_scalar(cv, ph["pj"][:, s, 0:SEQ], col[:, w:w + 1], c("conv_b", j),
                                          ALU.mult, ALU.add).then_inc(ph["y"], 1)
                        n += 1
                        for k in range(1, DCONV):
                            dve.wait_ge(ph["y"], n)
                            last = dve.scalar_tensor_tensor(out=cv, in0=ph["pj"][:, s, k:k + SEQ],
                                                            scalar=col[:, w + k:w + k + 1], in1=cv,
                                                            op0=ALU.mult, op1=ALU.add)
                            if k < DCONV - 1:
                                last.then_inc(ph["y"], 1)
                                n += 1
                        last.then_inc(ph["convd"], 1)
                    for j in range(MT):
                        s = j % 2
                        dve.wait_ge(ph["e_chain"], 2 * j + 1)
                        if j >= 2:
                            dve.wait_ge(ph["dt"], j - 1)
                        dve.tensor_scalar(ph["rl"][:, s, :], bank[s][:, :], c("dt_b", j), 0.0, ALU.add, ALU.max)\
                            .then_inc(ph["relu"], 1)
                        dve.wait_ge(ph["relu"], j + 1)
                        dve.wait_ge(ph["conv"], j + 1)
                        if j >= 2:
                            dve.wait_ge(ph["decay"], j - 1)
                        dve.tensor_tensor(ph["dtv"][:, s, :], ph["rl"][:, s, :], ph["el"][:, s, :], ALU.add)\
                            .then_inc(ph["dt"], 1)
                        dve.wait_ge(ph["dt"], j + 1)
                        dve.scalar_tensor_tensor(out=ph["drv"][:, s, :], in0=ph["dtv"][:, s, :], scalar=c("Bp", j),
                                                 in1=ph["Xs"][:, j, :], op0=ALU.mult, op1=ALU.mult)\
                            .then_inc(ph["drive"], 1)
                        dve.wait_ge(ph["drive"], j + 1)
                        dve.wait_ge(ph["decay"], j + 1)
                        dve.tensor_tensor_scan(ph["st"][:, s, :], ph["dec"][:, s, :], ph["drv"][:, s, :], 0.0,
                                               ALU.mult, ALU.add).then_inc(ph["scan"], 1)
                        dve.wait_ge(ph["scan"], j + 1)
                        dve.wait_ge(ph["skip"], j + 1)
                        dve.scalar_tensor_tensor(out=ph["st"][:, s, :], in0=ph["st"][:, s, :], scalar=c("Cp", j),
                                                 in1=ph["sk"][:, s, :], op0=ALU.mult, op1=ALU.add)\
                            .then_inc(ph["y"], 1)
                        n += 1
                        dve.wait_ge(ph["y"], n)
                        if j >= 2:
                            dve.wait_ge(ph["out_mm"], j - 1)
                        dve.tensor_tensor(ph["cb"][:, s, :], ph["st"][:, s, :], ph["gate"][:, j, :], ALU.mult)\
                            .then_inc(ph["comb"], 1)
                    dve.wait_ge(ph["out_mm"], MT)
                    for t in range(TT):
                        dve.tensor_tensor(X[:, t, :], bank[4 + t][:, :], X[:, t, :], ALU.add)\
                            .then_inc(ph["x_out"], 1)

                @block.gpsimd
                def _(pool):
                    for s in range(2):
                        pool.memset(ph["pj"][:, s, 0:DCONV - 1], 0.0).then_inc(ph["pads"], 1)
                    for j in range(MT):
                        pool.wait_ge(ph["sig"], j + 1)
                        pool.tensor_tensor(ph["Xs"][:, j, :], ph["cv"][:, j % 2, :], ph["sg"][:, j % 2, :], ALU.mult)\
                            .then_inc(ph["act_x"], 1)
                    pool.wait_ge(ph["act_x"], MT)
                    for j in range(MT):
                        if j >= 2:
                            pool.wait_ge(ph["comb"], j - 1)
                        pool.tensor_scalar(ph["sk"][:, j % 2, :], ph["Xs"][:, j, :], c("Dp", j), None, ALU.mult)\
                            .then_inc(ph["skip"], 1)

        setup()
        with nc.Fori(0, BATCH) as b:
            attention(b)
            ffn("ffn1", load_mix_weights)
            mixer()
            ffn("ffn2", load_att_weights, store_to=b)


def kernel(**inputs):
    import numpy as np
    import concourse.bacc as bacc
    from concourse.bass_utils import run_bass_kernel_spmd

    a = {k: np.asarray(v) for k, v in inputs.items()}
    A, B, C = "L0_attn_a_", "L0_attn_b_", "L0_ffn_"

    def columns(v, width):
        return v.reshape(width, P).T

    def feature_first(w):
        return w.reshape((GROUPS, HG, HD) + w.shape[1:]).swapaxes(1, 2).reshape(w.shape)

    conv_w = a[B + "conv_w"].reshape(MT, P, DCONV).transpose(1, 0, 2).reshape(P, MT * DCONV)
    gates = [a[A + g + "_gate"] for g in ("truth", "balance", "order", "justice", "harmony")]
    cols = np.concatenate(
        [columns(feature_first(a[A + "bq"]), KT), columns(feature_first(a[A + "bk"]), KT), columns(a[A + "bv"], KT),
         columns(a[C + "gate_scale"], FT), columns(a[C + "up_scale"], FT), conv_w,
         columns(a[B + "conv_b"], MT), columns(a[B + "dt_w"], MT),
         columns(np.repeat(a[B + "dt_b"], HDIM), MT)]
        + [columns(a[B + n], MT) for n in ("A_log", "Bp", "Cp", "Dp")]
        + [np.broadcast_to(g, (P, 1)) for g in gates], axis=1)
    rows = np.broadcast_to(np.stack([a[A + "bo"], a[C + "down_scale"]]), (P, 2, DM))
    i = np.arange(P)
    arrays = {
        "x": a[A + "hidden_states"],
        "wq": feature_first(a[A + "Wq"]).T, "wk": feature_first(a[A + "Wk"]).T, "wv": a[A + "Wv"].T, "wo": a[A + "Wo"].T,
        "w_gate": a[C + "gate_w"], "w_up": a[C + "up_w"], "w_down": a[C + "down_w"],
        "w_in": a[B + "in_proj_w"].T, "w_mg": a[B + "gate_proj_w"].T, "w_out": a[B + "out_proj_w"].T,
        "cols": cols, "rows": rows,
        "identity": np.eye(P, dtype=np.float32),
        "head_mask": (i[:, None] // HDIM == i[None, :] // HDIM).astype(np.float32),
        "group_mask": (i[:, None] % HG == np.arange(HG)[None, :]).astype(np.float32),
        "key_pos": np.tile((np.arange(SEQ) * ORDER_STEP).astype(np.float32), (3 * HG, 1)),
    }
    arrays = {k: np.ascontiguousarray(v) for k, v in arrays.items()}
    nc = bacc.Bacc("TRN2", target_bir_lowering=False, num_devices=1)
    args = [nc.dram_tensor(k, v.shape, mybir.dt.from_np(v.dtype), kind="ExternalInput").ap()
            for k, v in arrays.items()]
    out = nc.dram_tensor("out", (BATCH, SEQ, DM), F32, kind="ExternalOutput").ap()
    hybrid_layers(nc, *args, out)
    r = run_bass_kernel_spmd(nc, [arrays], core_ids=[0])
    return r.results[0]["out"]
```

```python
from contextlib import ExitStack, contextmanager
import math

import concourse.bass as bass
from concourse import mybir

F32 = mybir.dt.float32
F32R = mybir.dt.float32r
I32 = mybir.dt.int32
FP8 = mybir.dt.float8e4
BF16 = mybir.dt.bfloat16
ALU = mybir.AluOpType
ACT = mybir.ActivationFunctionType
AX = mybir.AxisListType.X

P = 128
BATCH, SEQ, DM = 4, 512, 512
HEADS, HD = 16, 32
TT = SEQ // P
KT = DM // P
HG = P // HD
GROUPS = HEADS // HG
GT = HG * TT
NS = HEADS * TT
FF = 1536
FT = FF // P
INNER, HDIM, DCONV = 1024, 64, 4
MT = INNER // P
EPS = 1e-5
ORDER_STEP = 0.05 / SEQ

KSTK = 3 * HD
ROW_R = KSTK
ROW_O = KSTK + 2
KALL = KSTK + 4
NPT = 4
ROW_TERMS = 64 + 3 * HG
LAG = 24

COLS = {}
_at = 0
for _n, _w in (("bq", KT), ("bk", KT), ("gate_scale", FT), ("up_scale", FT), ("conv_w", MT * DCONV),
               ("conv_b", MT), ("dt_w", MT), ("dt_b", MT), ("A_log", MT), ("Bp", MT), ("Cp", MT),
               ("Dp", MT), ("gates", 5)):
    COLS[_n] = _at
    _at += _w
NCOL = _at


def hybrid_layers(nc, x, wq, wk, wv, wo, w_gate, w_up, w_down, w_in, w_mg, w_out, cols, rows,
                  identity, head_mask, group_mask, key_pos, out):
    ctx = ExitStack()
    with ctx:
        def sb(name, shape, dt=F32, c=ctx):
            return c.enter_context(nc.sbuf_tensor(name, shape, dt))

        bank = [ctx.enter_context(nc.psum_tensor(f"bank{i}", [P, 512], F32)) for i in range(8)]

        X = sb("X", [P, TT, DM])
        ffnw = sb("ffnw", [P, FT, 3 * 512], BF16)
        wreg = sb("wreg", [P, 3 * KT * INNER])
        col = sb("col", [P, NCOL])
        row = sb("row", [P, 3, 512])
        ident = sb("ident", [P, P])
        hmask = sb("hmask", [P, P])
        gmask = sb("gmask", [P, HG])
        negA = sb("negA", [P, MT])
        coef = sb("coef", [P, 8])
        ones32 = sb("ones32", [P, HD])
        row_terms = sb("row_terms", [ROW_TERMS, SEQ], F32R)
        ones_row, order_h, order_l = (row_terms[q:q + 3 * HG, :] for q in (0, 32, 64))
        C_T, C_B, C_O, C_J, C_H, C_A, C_RA = range(7)

        att_w = wreg[:, 0:4 * KT * DM].rearrange("p (m k n) -> p m k n", m=4, k=KT)
        att_tail = wreg[:, 4 * KT * DM:]
        nT_att = att_tail[:, 0:KT * SEQ].rearrange("p (k n) -> p k n", k=KT)
        V = att_tail[:, KT * SEQ:].rearrange("p (t n) -> p t n", t=TT)
        mix_in = wreg[:, 0:KT * INNER].rearrange("p (k n) -> p k n", k=KT)
        mix_gate = wreg[:, KT * INNER:2 * KT * INNER].rearrange("p (k n) -> p k n", k=KT)
        mix_out = wreg[:, 2 * KT * INNER:].rearrange("p (j n) -> p j n", j=MT)

        def c(name, j=0):
            return col[:, COLS[name] + j:COLS[name] + j + 1]

        def load_att_weights(sp, done):
            for m, w in enumerate((wq, wk, wv, wo)):
                sp.dma_start(att_w[:, m], w.rearrange("(k p) n -> p k n", p=P)).then_inc(done, 16)

        def load_mix_weights(sp, done):
            for dst, w in ((mix_in, w_in), (mix_gate, w_mg), (mix_out, w_out)):
                sp.dma_start(dst, w.rearrange("(k p) n -> p k n", p=P)).then_inc(done, 16)

        def move(eng, dst, src, done):
            eng.dma_start(dst.bitcast(F32), src.bitcast(F32)).then_inc(done, 16)

        @contextmanager
        def phase(name, sems, buffers):
            with ExitStack() as stack:
                ph = {n: stack.enter_context(nc.semaphore(f"{name}_{n}")) for n in sems}
                ph.update({n: sb(f"{name}_{n}", shape, dt, stack) for n, (shape, dt) in buffers.items()})
                with nc.Block() as block:
                    yield ph, block
                for n in sems:
                    nc.sync.sem_clear(ph[n])
                nc.all_engine_barrier()

        LN_SEMS = ["ln_chain", "normed", "turned"]
        LN_BUFS = {"bn": ([P, TT, 6], F32), "mv": ([P, TT, 2], F32), "ln_v": ([P, TT], F32),
                   "ln_y": ([P, TT], F32), "ln_t": ([P, TT], F32), "N": ([P, TT, DM], F32)}

        def layernorm_vector(dve, ph, x_loaded=None):
            n = 0
            if x_loaded is not None:
                dve.wait_ge(x_loaded, 16 * TT)
            for t in range(TT):
                dve.bn_stats(ph["bn"][:, t, :], X[:, t, :]).then_inc(ph["ln_chain"], 1)
            n += TT
            dve.wait_ge(ph["ln_chain"], n)
            for t in range(TT):
                dve.bn_aggr(ph["mv"][:, t, :], ph["bn"][:, t, :]).then_inc(ph["ln_chain"], 1)
            n += TT
            dve.wait_ge(ph["ln_chain"], n)
            v, y, w = ph["ln_v"][:, :], ph["ln_y"][:, :], ph["ln_t"][:, :]
            dve.tensor_scalar(v, ph["mv"][:, :, 1], EPS, None, ALU.add).then_inc(ph["ln_chain"], 1)
            n += 1
            dve.wait_ge(ph["ln_chain"], n)
            dve.tensor_scalar(w.bitcast(I32), v.bitcast(I32), 1, None,
                              ALU.logical_shift_right).then_inc(ph["ln_chain"], 1)
            n += 1
            dve.wait_ge(ph["ln_chain"], n)
            dve.tensor_scalar(y.bitcast(I32), w.bitcast(I32), -1, 0x5f3759df,
                              ALU.mult, ALU.add).then_inc(ph["ln_chain"], 1)
            n += 1
            for _ in range(3):
                dve.wait_ge(ph["ln_chain"], n)
                dve.tensor_tensor(w, y, y, ALU.mult).then_inc(ph["ln_chain"], 1)
                dve.wait_ge(ph["ln_chain"], n + 1)
                dve.scalar_tensor_tensor(out=w, in0=w, scalar=-0.5, in1=v, op0=ALU.mult,
                                         op1=ALU.mult).then_inc(ph["ln_chain"], 1)
                dve.wait_ge(ph["ln_chain"], n + 2)
                dve.scalar_tensor_tensor(out=y, in0=w, scalar=1.5, in1=y, op0=ALU.add,
                                         op1=ALU.mult).then_inc(ph["ln_chain"], 1)
                n += 3
            dve.wait_ge(ph["ln_chain"], n)
            for t in range(TT):
                dve.tensor_scalar(ph["N"][:, t, :], X[:, t, :], ph["mv"][:, t, 0:1], y[:, t:t + 1],
                                  ALU.subtract, ALU.mult).then_inc(ph["normed"], 1)

        def layernorm_turn(pe, ph):
            for k in range(KT):
                for t in range(TT):
                    if k == 0:
                        pe.wait_ge(ph["normed"], t + 1)
                    last = pe.transpose(bank[k][:, t * P:(t + 1) * P], ph["N"][:, t, k * P:(k + 1) * P],
                                        ident[:, :])
                last.then_inc(ph["turned"], 1)

        def setup():
            sems = ["loaded", "staged0", "staged1", "weights", "chain", "ones", "gate_exp", "tile_done"]
            bufs = {"stage": ([P, 2, 3 * 512], F32), "body": ([P, 3 * 512], FP8), "above": ([P, 3 * 512], FP8),
                    "below": ([P, 3 * 512], FP8), "far": ([P, 3 * 512], F32), "sg": ([P, 5], F32),
                    "pos": ([ROW_TERMS, SEQ], F32), "o32": ([ROW_TERMS, SEQ], F32), "one": ([3 * HG, SEQ], F32)}
            with phase("setup", sems, bufs) as (ph, block):
                staged = (ph["staged0"], ph["staged1"])

                @block.sync
                def _(sp):
                    for dst, src in ((col, cols), (row, rows), (ident, identity), (hmask, head_mask),
                                     (gmask, group_mask), (ph["pos"], key_pos)):
                        sp.dma_start(dst[:], src).then_inc(ph["loaded"], 16)
                    for i in range(FT):
                        if i >= 2:
                            sp.wait_ge(ph["tile_done"], i - 1)
                        f = slice(i * P, (i + 1) * P)
                        st = ph["stage"][:, i % 2].rearrange("p (m k n) -> p m k n", m=3, k=KT)
                        for m, w in enumerate((w_gate, w_up)):
                            sp.dma_start(st[:, m], w.rearrange("(k p) n -> p k n", p=P)[:, :, f])\
                                .then_inc(staged[i % 2], 16)
                        sp.dma_start(ph["stage"][:, i % 2, 1024:1536], w_down[f, :]).then_inc(staged[i % 2], 16)
                    load_att_weights(sp, ph["weights"])
                    sp.wait_ge(ph["weights"], 16 * 4)

                @block.vector
                def _(dve):
                    n = 0

                    def chained(ins):
                        nonlocal n
                        n += 1
                        ins.then_inc(ph["chain"], 1)
                        dve.wait_ge(ph["chain"], n)

                    chained(dve.memset(ones32[:, :], 1.0))
                    chained(dve.memset(ph["one"][:, :], 1.0))
                    dve.wait_ge(ph["loaded"], 16 * 6)
                    dve.wait_ge(ph["gate_exp"], 1)
                    chained(dve.tensor_scalar(ph["sg"][:, :], ph["sg"][:, :], 1.0, None, ALU.add))
                    chained(dve.reciprocal(ph["sg"][:, :], ph["sg"][:, :]))
                    for k, (g, f) in {C_T: (0, -0.01), C_B: (1, 0.1 / math.log(SEQ)), C_O: (2, 1.0),
                                      C_J: (3, 0.1), C_H: (4, -0.1 / (SEQ - 1))}.items():
                        chained(dve.tensor_scalar(coef[:, k:k + 1], ph["sg"][:, g:g + 1], f, None, ALU.mult))
                    chained(dve.tensor_scalar(coef[:, C_A:C_A + 1], coef[:, C_J:C_J + 1], -1.0, 1.0,
                                              ALU.mult, ALU.add))
                    chained(dve.reciprocal(coef[:, C_RA:C_RA + 1], coef[:, C_A:C_A + 1]))
                    chained(dve.tensor_scalar(ph["o32"][:, :], ph["pos"][:, :], coef[0:ROW_TERMS, C_O:C_O + 1],
                                              coef[0:ROW_TERMS, C_RA:C_RA + 1], ALU.mult, ALU.mult))
                    chained(dve.tensor_copy(row_terms[:, :], ph["o32"][:, :]))
                    chained(dve.tensor_tensor(order_l, ph["o32"][64:ROW_TERMS, :], order_l.bitcast(F32),
                                              ALU.subtract))
                    chained(dve.tensor_copy(ones_row, ph["one"][:, :]))
                    dve.wait_ge(ph["gate_exp"], 2)
                    chained(dve.tensor_scalar(negA[:, :], negA[:, :], -1.0, None, ALU.mult))
                    for i in range(FT):
                        dve.wait_ge(staged[i % 2], 48 * (i // 2 + 1))
                        w = ph["stage"][:, i % 2, :]
                        dve.tensor_scalar(ph["body"][:, :], w, 128.0, -128.0, ALU.min, ALU.max,
                                          saturate=False).then_inc(ph["chain"], 1)
                        dve.tensor_scalar(ph["above"][:, :], w, 128.0, 0.5, ALU.max, ALU.mult,
                                          saturate=False).then_inc(ph["chain"], 1)
                        dve.tensor_scalar(ph["below"][:, :], w, -128.0, 0.5, ALU.min, ALU.mult,
                                          saturate=False).then_inc(ph["tile_done"], 1)
                        n += 2
                        dve.wait_ge(ph["chain"], n)
                        dve.wait_ge(ph["tile_done"], i + 1)
                        chained(dve.tensor_tensor(ph["far"][:, :], ph["above"][:, :], ph["below"][:, :], ALU.add))
                        chained(dve.scalar_tensor_tensor(out=ffnw[:, i, :], in0=ph["far"][:, :], scalar=2.0,
                                                         in1=ph["body"][:, :], op0=ALU.mult, op1=ALU.add))

                @block.scalar
                def _(act):
                    act.wait_ge(ph["loaded"], 16 * 6)
                    g = COLS["gates"]
                    act.activation(ph["sg"][:, :], col[:, g:g + 5], ACT.Exp, scale=-1.0).then_inc(ph["gate_exp"], 1)
                    a = COLS["A_log"]
                    act.activation(negA[:, :], col[:, a:a + MT], ACT.Exp).then_inc(ph["gate_exp"], 1)

        def attention(b):
            order = ["q0", "k0", "s0", "q1"] + ["k1", "v0", "v1", "s1", "v2", "q2", "v3"]
            for g in range(1, GROUPS + 1):
                if g + 1 < GROUPS:
                    order += [f"k{g + 1}"]
                if g >= 1:
                    order += [f"r{g - 1}"]
                if g + 1 < GROUPS:
                    order += [f"s{g + 1}"]
                if g + 2 < GROUPS:
                    order += [f"q{g + 2}"]
            order += [f"o{t}" for t in range(TT)]
            DIFF, PROJ, PROB, OUT, SUM = 3, 4, 5, 6, 7
            place = {"q0": 4, "k0": 6, "s0": 7, "v0": 5, "v1": 6, "v2": 7, "v3": 5,
                     "o0": 0, "o1": 1, "o2": 2, "o3": 3}
            I_K, I_R, I_S, I_Q = 0, 4, 7, 12

            def at(name):
                return bank[place.get(name, PROJ)]

            def score_bank(n):
                return bank[n % 3]

            def act_differs(n):
                return n < LAG or n % 2 == 0

            def differed(eng, n):
                on_act = sum(act_differs(j) for j in range(n))
                if on_act:
                    eng.wait_ge(ph["diff_act"], on_act)
                if n > on_act:
                    eng.wait_ge(ph["diff_dve"], n - on_act)

            two, three = NS + 1 - LAG, NS + I_R + 2 - LAG

            def prob_bank(m):
                return bank[PROB if m < two or m % 2 == 0 else DIFF if m < three else PROJ]

            sems = LN_SEMS + ["x_in", "nt_act", "nt_dve", "filled", "v_ready",
                              "q_ready", "k_ready", "k2_ready", "dk_ready", "mean_w", "q_parts", "k_parts", "d_parts",
                              "const_rows", "stk0", "stk1", "score", "maxed", "exped", "ent", "diff", "diff_act",
                              "diff_dve", "prob_mm", "prob", "pv", "scaled", "chain", "stat_read", "lns",
                              "rz_ready", "shift", "shift_h", "shift_l", "shift_rows", "xb", "x_out"]
            bufs = dict(LN_BUFS)
            bufs |= {"k32": ([P, SEQ], F32), "tmp": ([P, 6, SEQ], F32R), "Qs": ([P, 3, HG, SEQ], F32R),
                     "Ks": ([P, 3, HG, SEQ], F32R), "Ds": ([KSTK, 2, HG, SEQ], F32R), "E": ([P, 2, SEQ], F32),
                     "PT": ([P, NPT, SEQ], F32), "rz": ([P, SEQ], F32), "lnz": ([P, SEQ], F32),
                     "nmax": ([P, NS], F32), "Z": ([P, NS], F32), "U": ([P, NS], F32), "Ab": ([P, NS], F32),
                     "stat": ([P, GROUPS, 2, TT, HG], F32), "ksum": ([P, GROUPS], F32),
                     "meanw": ([P, GROUPS, HG], F32), "w": ([P, 6, GT], F32), "r": ([P, GT], F32),
                     "rh": ([GT, P], F32R), "rl": ([GT, P], F32R)}
            with phase("att", sems, bufs) as (ph, block):
                OT = ph["N"]
                q32, dk, k2 = ph["N"][:, 1, :], ph["N"][:, 2, :], ph["N"][:, 3, :]
                QH, QL, KH, KL, DH, DL = range(6)

                def stacked(eng, g):
                    eng.wait_ge((ph["stk0"], ph["stk1"])[g % 2], 16 * 9 * (g // 2 + 1))

                def filled(eng, name):
                    eng.wait_ge(ph["filled"], order.index(name) + 1)

                @block.sync
                def _(sp):
                    for t in range(TT):
                        sp.dma_start(X[:, t, :], x[b, t * P:(t + 1) * P, :]).then_inc(ph["x_in"], 16)

                    def const_rows():
                        for dst, row0, src in (("Ks", ROW_R, ones_row), ("Ks", ROW_R + 1, ones_row),
                                               ("Ks", ROW_O, order_h), ("Ks", ROW_O + 1, order_l),
                                               ("Qs", ROW_O, ones_row), ("Qs", ROW_O + 1, ones_row)):
                            move(sp, ph[dst][row0:row0 + 1], src, ph["const_rows"])

                    def stack_up(g):
                        if g >= 2:
                            sp.wait_ge(ph["diff"], GT * (g - 1))
                        if g >= 3:
                            sp.wait_ge(ph["prob_mm"], GT * (g - 2))
                        for dst, parts, split in ((ph["Qs"][:, g % 3], (QH, QH, QL), ph["q_parts"]),
                                                  (ph["Ks"][:, g % 3], (KH, KL, KH), ph["k_parts"]),
                                                  (ph["Ds"][:, g % 2], (DH, DL, DH), ph["d_parts"])):
                            sp.wait_ge(split, 2 * (g + 1))
                            for i, part in enumerate(parts):
                                move(sp, dst[HD * i:HD * (i + 1)], ph["tmp"][:, part, :],
                                     (ph["stk0"], ph["stk1"])[g % 2])

                    def shift_rows(g):
                        sp.wait_ge(ph["shift_h"], g + 1)
                        move(sp, ph["Qs"][ROW_R:ROW_R + 1, g % 3], ph["rh"][:, :], ph["shift_rows"])
                        sp.wait_ge(ph["shift_l"], g + 1)
                        move(sp, ph["Qs"][ROW_R + 1:ROW_R + 2, g % 3], ph["rl"][:, :], ph["shift_rows"])

                    stack_up(0)
                    const_rows()
                    stack_up(1)
                    for g in range(GROUPS):
                        shift_rows(g)
                        if g + 2 < GROUPS:
                            stack_up(g + 2)
                    sp.wait_ge(ph["shift_rows"], 32 * GROUPS)

                @block.tensor
                def _(pe):
                    layernorm_turn(pe, ph)
                    pe.wait_ge(ph["nt_act"], 2)
                    pe.wait_ge(ph["nt_dve"], 2)

                    def project(g, name, m, ks=range(KT)):
                        for k in ks:
                            last = pe.matmul(at(f"{name}{g}")[:, :], att_w[:, m, k, g * P:(g + 1) * P],
                                             nT_att[:, k, :], start=(k == 0), stop=(k == KT - 1))
                        if k == KT - 1:
                            last.then_inc(ph["filled"], 1)

                    def key_stats(g, ts):
                        pe.wait_ge(ph["k2_ready"], g + 1)
                        pe.wait_ge(ph["q_ready"], g + 1)
                        pe.wait_ge(ph["mean_w"], g + 1)
                        to = at(f"s{g}")
                        for t in ts:
                            pe.matmul(to[:, HG * t:HG * (t + 1)], k2[:, t * P:(t + 1) * P], gmask[:, :],
                                      start=True, stop=True)
                            last = pe.matmul(to[:, GT + HG * t:GT + HG * (t + 1)], q32[:, t * P:(t + 1) * P],
                                             ph["meanw"][:, g, :], start=True, stop=True)
                        if t == TT - 1:
                            last.then_inc(ph["filled"], 1)

                    def score(n):
                        g, i = divmod(n, GT)
                        h, t = divmod(i, TT)
                        if i == 0:
                            stacked(pe, g)
                        if n >= 3:
                            pe.wait_ge(ph["ent"], n - 2)
                        pe.matmul(score_bank(n)[:, :], ph["Qs"][0:KSTK, g % 3, h, t * P:(t + 1) * P],
                                  ph["Ks"][0:KSTK, g % 3, h, :], start=True, stop=True).then_inc(ph["score"], 1)

                    def difference(n):
                        g, i = divmod(n, GT)
                        h, t = divmod(i, TT)
                        if n >= 1:
                            differed(pe, n)
                        pe.matmul(bank[DIFF][:, :], ph["Qs"][0:KSTK, g % 3, h, t * P:(t + 1) * P],
                                  ph["Ds"][:, g % 2, h, :], start=True, stop=True).then_inc(ph["diff"], 1)

                    def probability(m):
                        gm, im = divmod(m, GT)
                        h, k = divmod(im, TT)
                        if m == 0:
                            pe.wait_ge(ph["const_rows"], 16 * 6)
                            pe.wait_ge(ph["v_ready"], TT)
                        if im == 0:
                            pe.wait_ge(ph["shift_rows"], 32 * (gm + 1))
                        if m == two:
                            differed(pe, NS)
                        if m == three + 1:
                            pe.wait_ge(ph["shift_l"], GROUPS)
                        if m >= 1:
                            pe.wait_ge(ph["prob"], m - 1 if m > two else m)
                        pe.matmul(prob_bank(m)[:, :], ph["Ks"][0:KALL, gm % 3, h, k * P:(k + 1) * P],
                                  ph["Qs"][0:KALL, gm % 3, h, :], start=True, stop=True).then_inc(ph["prob_mm"], 1)

                    def weigh(m):
                        gm, im = divmod(m, GT)
                        h, k = divmod(im, TT)
                        pe.wait_ge(ph["prob"], m + 1)
                        if im == 0 and gm >= 1:
                            pe.wait_ge(ph["scaled"], gm)
                        hs = slice(HD * h, HD * (h + 1))
                        vs = slice((gm * HG + h) * HD, (gm * HG + h + 1) * HD)
                        pe.matmul(bank[OUT][hs, :], V[:, k, vs], ph["PT"][:, m % NPT, :], start=(k == 0),
                                  stop=(k == TT - 1), tile_position=(0, HD * h))
                        hs = (HD * h + P // 2) % P
                        pe.matmul(bank[SUM][hs:hs + HD, :], ones32[:, :], ph["PT"][:, m % NPT, :], start=(k == 0),
                                  stop=(k == TT - 1), tile_position=(0, hs)).then_inc(ph["pv"], 1)

                    def output(t, g):
                        pe.wait_ge(ph["scaled"], g + 1)
                        last = pe.matmul(at(f"o{t}")[:, :], OT[:, g, t * P:(t + 1) * P],
                                         att_w[:, 3, g, :], start=(g == 0), stop=(g == GROUPS - 1))
                        if g == GROUPS - 1:
                            last.then_inc(ph["filled"], 1)

                    def value(t, k):
                        if k == 0 and t == TT - 1:
                            pe.wait_ge(ph["v_ready"], 1)
                        elif k == 0 and t == 2:
                            pe.wait_ge(ph["stat_read"], 1)
                        last = pe.matmul(at(f"v{t}")[:, :], nT_att[:, k, t * P:(t + 1) * P],
                                         att_w[:, 2, k, :], start=(k == 0), stop=(k == KT - 1))
                        if k == KT - 1:
                            last.then_inc(ph["filled"], 1)

                    project(0, "q", 0)
                    project(0, "k", 1)
                    key_stats(0, range(TT))
                    project(1, "q", 0)
                    score(0)
                    score(1)
                    for n in range(NS + LAG + 1):
                        g, i = divmod(n, GT)
                        m = n - LAG
                        if 0 <= m < NS:
                            probability(m)
                        if n + 2 < NS:
                            score(n + 2)
                        if m >= GT and (m - 1) % GT == NPT - 2:
                            for late in range(m - NPT + 1, m - 1):
                                weigh(late)
                        if m >= 1 and (m <= GT or (m - 1) % GT >= NPT - 2):
                            weigh(m - 1)
                        if I_K <= i < I_K + KT and g + 1 < GROUPS:
                            if i == I_K:
                                pe.wait_ge(ph["q_ready"], g + 2)
                            project(g + 1, "k", 1, [i - I_K])
                        if i == I_R and 1 <= g <= GROUPS:
                            pe.wait_ge(ph["shift"], g)
                            if g + 1 < GROUPS:
                                pe.wait_ge(ph["k_ready"], g + 2)
                            pe.transpose(at(f"r{g - 1}")[0:GT, 0:P], ph["r"][:, :], ident[:, :])\
                                .then_inc(ph["filled"], 1)
                        if I_S <= i < I_S + 2 and g + 1 < GROUPS:
                            if g >= 1:
                                pe.wait_ge(ph["shift_l"], g)
                            key_stats(g + 1, range(2 * (i - I_S), 2 * (i - I_S + 1)))
                        if I_Q <= i < I_Q + KT and g + 2 < GROUPS:
                            if i == I_Q:
                                pe.wait_ge(ph["stat_read"], g + 2)
                            project(g + 2, "q", 0, [i - I_Q])
                        if g == 0:
                            value(*divmod(i, KT))
                        if n < NS:
                            difference(n)
                        e = n - (NS + 1)
                        if e == 0:
                            pe.wait_ge(ph["ent"], NS)
                        if 0 <= e < 2 * TT:
                            output(e // 2, e % 2)
                        e = m - (NS - GT + 4)
                        if 0 <= e < TT:
                            output(e, 2)
                    for t in range(TT):
                        output(t, GROUPS - 1)

                @block.scalar
                def _(act):
                    act.preload_act_table_set("natural_log_exp_and_others")
                    for k in (0, 2):
                        act.wait_ge(ph["turned"], k + 1)
                        act.activation(nT_att[:, k, :], bank[k][:, :], ACT.Copy).then_inc(ph["nt_act"], 1)

                    def key(g):
                        filled(act, f"k{g}")
                        if g >= 1:
                            act.wait_ge(ph["k_parts"], 2 * g)
                            act.wait_ge(ph["k2_ready"], g)
                            act.wait_ge(ph["dk_ready"], g)
                        act.activation(ph["k32"][:, :], at(f"k{g}")[:, :], ACT.Identity, bias=c("bk", g),
                                       accum_out=ph["ksum"][:, g:g + 1]).then_inc(ph["k_ready"], 1)

                    key(0)
                    for n in range(NS + LAG + 1):
                        g, i = divmod(n, GT)
                        if i == I_K + KT and g + 1 < GROUPS:
                            key(g + 1)
                        if i == I_R + 1 and 1 <= g <= GROUPS:
                            filled(act, f"r{g - 1}")
                            if g >= 2:
                                act.wait_ge(ph["shift_rows"], 32 * (g - 1))
                            act.activation(ph["rh"][:, :], at(f"r{g - 1}")[0:GT, 0:P], ACT.Copy)\
                                .then_inc(ph["shift_h"], 1)
                        if n < NS:
                            act.wait_ge(ph["maxed"], n + 1)
                            if n >= 2:
                                act.wait_ge(ph["ent"], n - 1)
                            act.activation(ph["E"][:, n % 2, :], score_bank(n)[:, :], ACT.Exp,
                                           bias=ph["nmax"][:, n:n + 1], accum_out=ph["Z"][:, n:n + 1])\
                                .then_inc(ph["exped"], 1)
                        if 1 <= n <= NS and act_differs(n - 1):
                            act.wait_ge(ph["diff"], n)
                            act.activation(bank[DIFF][:, :], bank[DIFF][:, :], ACT.Abs,
                                           accum_out=ph["Ab"][:, n - 1:n]).then_inc(ph["diff_act"], 1)
                        if i == 0 and 1 <= g <= GROUPS:
                            s = slice((g - 1) * GT, g * GT)
                            act.wait_ge(ph["exped"], GT * g)
                            act.activation(ph["w"][:, 0, :], ph["Z"][:, s], ACT.Ln).then_inc(ph["lns"], 1)
                            kn = ph["w"][:, 1, :].rearrange("p (h t) -> p t h", h=HG)
                            act.activation(kn, ph["stat"][:, g - 1, 0], ACT.Ln).then_inc(ph["lns"], 1)
                            act.wait_ge(ph["lns"], 3 * g - 1)
                            act.activation(ph["w"][:, 2, :], ph["w"][:, 1, :], ACT.Exp, scale=0.5).then_inc(ph["lns"], 1)
                        m = n - LAG
                        if m >= 1 and m % GT == 0:
                            act.wait_ge(ph["pv"], m)
                            act.activation(ph["lnz"][:, :], bank[SUM][:, :], ACT.Ln).then_inc(ph["rz_ready"], 1)
                            act.wait_ge(ph["rz_ready"], 3 * (m // GT) - 2)
                            if m > GT:
                                act.wait_ge(ph["scaled"], m // GT - 1)
                            for o, z in ((slice(0, 64), slice(64, P)), (slice(64, P), slice(0, 64))):
                                act.activation(ph["rz"][o, :], ph["lnz"][z, :], ACT.Exp, scale=-1.0)\
                                    .then_inc(ph["rz_ready"], 1)
                        if 0 <= m < NS:
                            act.wait_ge(ph["prob_mm"], m + 1)
                            if m >= NPT:
                                act.wait_ge(ph["pv"], m - NPT + 1)
                            act.activation(ph["PT"][:, m % NPT, :], prob_bank(m)[:, :], ACT.Exp,
                                           scale=coef[:, C_A:C_A + 1]).then_inc(ph["prob"], 1)

                @block.vector
                def _(dve):
                    layernorm_vector(dve, ph, ph["x_in"])
                    for k in (1, 3):
                        dve.wait_ge(ph["turned"], k + 1)
                        dve.tensor_copy(nT_att[:, k, :], bank[k][:, :]).then_inc(ph["nt_dve"], 1)

                    def split(g, full, hi, lo, done):
                        dve.tensor_copy(ph["tmp"][:, hi, :], full).then_inc(done, 1)
                        if g == 0:
                            dve.wait_ge(done, 1)
                            dve.tensor_tensor(ph["tmp"][:, lo, :], full, ph["tmp"][:, hi, :].bitcast(F32),
                                              ALU.subtract).then_inc(done, 1)

                    def query(g):
                        filled(dve, f"q{g}")
                        if g >= 1:
                            dve.wait_ge(ph["q_parts"], 2 * g)
                            filled(dve, f"s{g - 1}")
                        else:
                            dve.wait_ge(ph["turned"], KT)
                        dve.tensor_scalar(q32, at(f"q{g}")[:, :], c("bq", g), 1 / math.sqrt(HD),
                                          ALU.add, ALU.mult).then_inc(ph["q_ready"], 1)
                        dve.wait_ge(ph["q_ready"], g + 1)
                        if g >= 1:
                            stacked(dve, g - 1)
                        split(g, q32, QH, QL, ph["q_parts"])

                    def split_key(g):
                        dve.wait_ge(ph["k_ready"], g + 1)
                        dve.tensor_scalar(ph["meanw"][:, g, :], gmask[:, :], ph["ksum"][:, g:g + 1], 1 / SEQ,
                                          ALU.mult, ALU.mult).then_inc(ph["mean_w"], 1)
                        split(g, ph["k32"][:, :], KH, KL, ph["k_parts"])

                    def split_difference(g):
                        dve.wait_ge(ph["dk_ready"], g + 1)
                        split(g, dk, DH, DL, ph["d_parts"])

                    def stats(g):
                        filled(dve, f"s{g}")
                        src = at(f"s{g}")[:, 0:2 * GT].rearrange("p (m t h) -> p m t h", m=2, t=TT)
                        dve.tensor_scalar(ph["stat"][:, g, 0], src[:, 0], 1e-18, None, ALU.max)\
                            .then_inc(ph["chain"], 1)
                        dve.tensor_copy(ph["stat"][:, g, 1], src[:, 1]).then_inc(ph["stat_read"], 1)

                    query(0)
                    split_key(0)
                    split_difference(0)

                    def value(t):
                        filled(dve, f"v{t}")
                        dve.tensor_tensor(V[:, t, :], at(f"v{t}")[:, :], row[:, 2, :], ALU.add)\
                            .then_inc(ph["v_ready"], 1)

                    stats(0)
                    chain = 1

                    def chained(ins):
                        nonlocal chain
                        chain += 1
                        ins.then_inc(ph["chain"], 1)
                        dve.wait_ge(ph["chain"], chain)

                    def maximum(n):
                        dve.wait_ge(ph["score"], n + 1)
                        dve.tensor_reduce(ph["nmax"][:, n:n + 1], score_bank(n)[:, :], AX, ALU.max, negate=True)\
                            .then_inc(ph["maxed"], 1)

                    def shift_part(g, j):
                        s = slice(g * GT, (g + 1) * GT)
                        w = ph["w"]
                        knorm, ent, acc, top = w[:, 2, :], w[:, 3, :], w[:, 4, :], w[:, 5, :]
                        mean = ph["stat"][:, g, 1].rearrange("p t h -> p h t")
                        acc_ht = acc.rearrange("p (h t) -> p h t", h=HG)

                        def k_(j):
                            return coef[:, j:j + 1]

                        def add(out, x, factor, y, op=ALU.add):
                            return dve.scalar_tensor_tensor(out=out, in0=x, scalar=k_(factor), in1=y,
                                                            op0=ALU.mult, op1=op)

                        nonlocal chain
                        if j == 0:
                            dve.wait_ge(ph["ent"], GT * (g + 1))
                            dve.wait_ge(ph["lns"], 3 * (g + 1))
                            differed(dve, GT * (g + 1))
                        else:
                            dve.wait_ge(ph["chain"], chain)
                        chain += 1
                        if j == 0:
                            done = dve.reciprocal(ent, ph["Z"][:, s])
                        elif j == 1:
                            done = dve.tensor_tensor(ent, ent, ph["U"][:, s], ALU.mult)
                        elif j == 2:
                            done = dve.tensor_tensor(ent, w[:, 0, :], ent, ALU.subtract)
                        elif j == 3:
                            done = dve.tensor_scalar(acc, knorm, k_(C_T), None, ALU.mult)
                        elif j == 4:
                            done = add(acc, ent, C_B, acc)
                        elif j == 5:
                            done = add(acc_ht, mean, C_J, acc_ht)
                        elif j == 6:
                            done = add(acc, ph["Ab"][:, s], C_H, acc)
                        elif j == 7:
                            done = add(top, ph["nmax"][:, s], C_A, acc, ALU.subtract)
                        elif j == 8:
                            done = dve.tensor_tensor(acc, top, acc, ALU.add)
                        else:
                            if g >= 1:
                                dve.wait_ge(ph["shift_h"], g)
                            chain -= 1
                            dve.tensor_scalar(ph["r"][:, :], acc, k_(C_RA), None, ALU.mult).then_inc(ph["shift"], 1)
                            return
                        done.then_inc(ph["chain"], 1)

                    maximum(0)
                    for n in range(NS + LAG + 1):
                        g, i = divmod(n, GT)
                        shifting = 1 <= g <= GROUPS and i < 4
                        if i == 0 and g + 1 < GROUPS:
                            query(g + 1)
                        if n and n <= GT and n % KT == 0:
                            value(n // KT - 1)
                        if n + 1 < NS:
                            maximum(n + 1)
                        if shifting and i > 0:
                            shift_part(g - 1, 3 * i - 2)
                        if 1 <= n <= NS and not act_differs(n - 1):
                            dve.wait_ge(ph["diff"], n)
                            dve.tensor_reduce(ph["Ab"][:, n - 1:n], bank[DIFF][:, :], AX, ALU.add,
                                              apply_absolute_value=True).then_inc(ph["diff_dve"], 1)
                        if shifting and i > 0:
                            shift_part(g - 1, 3 * i - 1)
                        if n < NS:
                            dve.wait_ge(ph["exped"], n + 1)
                            dve.scalar_tensor_tensor(out=ph["E"][:, n % 2, :], in0=score_bank(n)[:, :],
                                                     scalar=ph["nmax"][:, n:n + 1], in1=ph["E"][:, n % 2, :],
                                                     op0=ALU.add, op1=ALU.mult, accum_out=ph["U"][:, n:n + 1])\
                                .then_inc(ph["ent"], 1)
                        if g + 1 < GROUPS:
                            if i == I_K + KT:
                                split_key(g + 1)
                            if i == I_K + KT + 1:
                                split_difference(g + 1)
                            if i == I_S + 2:
                                stats(g + 1)
                                chain += 1
                        if shifting:
                            shift_part(g - 1, 3 * i)
                        if i == I_R + 1 and 1 <= g <= GROUPS:
                            dve.wait_ge(ph["shift_h"], g)
                            if g >= 2:
                                dve.wait_ge(ph["shift_rows"], 32 * (g - 1))
                            dve.tensor_tensor(ph["rl"][:, :], at(f"r{g - 1}")[0:GT, 0:P],
                                              ph["rh"][:, :].bitcast(F32), ALU.subtract).then_inc(ph["shift_l"], 1)
                        m = n - LAG
                        if m >= 1 and m % GT == 0:
                            gm = m // GT - 1
                            dve.wait_ge(ph["pv"], m)
                            dve.wait_ge(ph["rz_ready"], 3 * (gm + 1))
                            dve.tensor_tensor(OT[:, gm, :], bank[OUT][:, :], ph["rz"][:, :], ALU.mult)\
                                .then_inc(ph["scaled"], 1)
                    for t in range(TT):
                        filled(dve, f"o{t}")
                        dve.wait_ge(ph["xb"], t + 1)
                        dve.tensor_tensor(X[:, t, :], at(f"o{t}")[:, :], X[:, t, :], ALU.add)\
                            .then_inc(ph["x_out"], 1)

                @block.gpsimd
                def _(pool):
                    for g in range(GROUPS):
                        def low(full, hi, lo, done):
                            if g >= 1:
                                pool.wait_ge(done, 2 * g + 1)
                                pool.tensor_tensor(ph["tmp"][:, lo, :], full, ph["tmp"][:, hi, :].bitcast(F32),
                                                   ALU.subtract).then_inc(done, 1)

                        if g >= 1:
                            stacked(pool, g - 1)
                            low(q32, QH, QL, ph["q_parts"])
                            filled(pool, f"s{g - 1}")
                        else:
                            pool.wait_ge(ph["turned"], KT)
                            pool.memset(dk[:, SEQ - 1:SEQ], 0.0)
                        pool.wait_ge(ph["k_ready"], g + 1)
                        pool.tensor_tensor(dk[:, 0:SEQ - 1], ph["k32"][:, 1:SEQ], ph["k32"][:, 0:SEQ - 1],
                                           ALU.subtract).then_inc(ph["dk_ready"], 1)
                        pool.tensor_tensor(k2, ph["k32"][:, :], ph["k32"][:, :], ALU.mult).then_inc(ph["k2_ready"], 1)
                        low(ph["k32"][:, :], KH, KL, ph["k_parts"])
                        low(dk, DH, DL, ph["d_parts"])
                        if g == 0:
                            for t in range(TT):
                                pool.wait_ge(ph["normed"], t + 1)
                                pool.tensor_tensor(X[:, t, :], X[:, t, :], row[:, 0, :], ALU.add).then_inc(ph["xb"], 1)

        def ffn(name, load_next, store_to=None):
            sems = LN_SEMS + ["n_high", "n_low", "w32", "gate_mm", "up_mm", "silu", "hid", "h_high", "h_low",
                              "down", "scaled", "x_out", "next_w", "stored"]
            bufs = dict(LN_BUFS)
            bufs |= {"nH": ([P, KT, SEQ], F32R), "nL": ([P, KT, SEQ], F32R), "wf": ([P, 3, 3, 512], F32R),
                     "sg": ([P, 2, SEQ], F32), "h32": ([P, 2, SEQ], F32), "hH": ([P, 3, SEQ], F32R),
                     "hL": ([P, 3, SEQ], F32R), "y": ([P, 2, 512], F32)}
            with phase(name, sems, bufs) as (ph, block):
                @block.sync
                def _(sp):
                    load_next(sp, ph["next_w"])
                    if store_to is not None:
                        for t in range(TT):
                            sp.wait_ge(ph["x_out"], t + 1)
                            sp.dma_start(out[store_to, t * P:(t + 1) * P, :], X[:, t, :]).then_inc(ph["stored"], 16)
                        sp.wait_ge(ph["stored"], 16 * TT)
                        sp.wait_ge(ph["next_w"], 16 * 4)
                    else:
                        sp.wait_ge(ph["next_w"], 16 * 3)

                @block.tensor
                def _(pe):
                    layernorm_turn(pe, ph)
                    pe.wait_ge(ph["n_low"], KT)
                    def up(i):
                        for j, (done, used) in enumerate(((ph["gate_mm"], ph["silu"]), (ph["up_mm"], ph["hid"]))):
                            if i >= 2:
                                pe.wait_ge(used, i - 1)
                            w = ph["wf"][:, i % 3, j, :].rearrange("p (k n) -> p k n", k=KT)
                            for k in range(KT):
                                for part in (ph["nH"], ph["nL"]):
                                    last = pe.matmul(bank[2 * j + i % 2][:, :], w[:, k, :], part[:, k, :],
                                                     start=(k == 0 and part is ph["nH"]),
                                                     stop=(k == KT - 1 and part is ph["nL"]))
                            last.then_inc(done, 1)

                    def down(i):
                        pe.wait_ge(ph["h_low"], i + 1)
                        for t in range(TT):
                            for part in (ph["hH"], ph["hL"]):
                                last = pe.matmul(bank[4 + t][:, :], part[:, i % 3, t * P:(t + 1) * P],
                                                 ph["wf"][:, i % 3, 2, :], start=(i == 0 and part is ph["hH"]),
                                                 stop=(i == FT - 1 and part is ph["hL"]))
                        last.then_inc(ph["down"], 1)

                    for i in range(FT):
                        pe.wait_ge(ph["w32"], i + 1)
                        up(i)
                        if i >= 1:
                            down(i - 1)
                    down(FT - 1)

                @block.scalar
                def _(act):
                    def widen(i):
                        if i >= 3:
                            act.wait_ge(ph["down"], i - 2)
                        act.activation(ph["wf"][:, i % 3].rearrange("p m n -> p (m n)"), ffnw[:, i, :], ACT.Copy)\
                            .then_inc(ph["w32"], 1)

                    widen(0)
                    widen(1)
                    for k in range(KT):
                        act.wait_ge(ph["turned"], k + 1)
                        act.activation(ph["nH"][:, k, :], bank[k][:, :], ACT.Copy).then_inc(ph["n_high"], 1)
                    for i in range(FT):
                        act.wait_ge(ph["gate_mm"], i + 1)
                        if i >= 2:
                            act.wait_ge(ph["hid"], i - 1)
                        act.activation(ph["sg"][:, i % 2, :], bank[i % 2][:, :], ACT.Silu,
                                       scale=c("gate_scale", i)).then_inc(ph["silu"], 1)
                        if i + 2 < FT:
                            widen(i + 2)

                @block.vector
                def _(dve):
                    layernorm_vector(dve, ph)
                    for k in range(KT):
                        dve.wait_ge(ph["n_high"], k + 1)
                        dve.tensor_tensor(ph["nL"][:, k, :], bank[k][:, :], ph["nH"][:, k, :].bitcast(F32),
                                          ALU.subtract).then_inc(ph["n_low"], 1)
                    for i in range(FT):
                        dve.wait_ge(ph["up_mm"], i + 1)
                        dve.wait_ge(ph["silu"], i + 1)
                        dve.scalar_tensor_tensor(out=ph["h32"][:, i % 2, :], in0=bank[2 + i % 2][:, :],
                                                 scalar=c("up_scale", i), in1=ph["sg"][:, i % 2, :],
                                                 op0=ALU.mult, op1=ALU.mult).then_inc(ph["hid"], 1)
                        dve.wait_ge(ph["hid"], i + 1)
                        if i >= 3:
                            dve.wait_ge(ph["down"], i - 2)
                        dve.tensor_copy(ph["hH"][:, i % 3, :], ph["h32"][:, i % 2, :]).then_inc(ph["h_high"], 1)
                        dve.wait_ge(ph["h_high"], i + 1)
                        dve.tensor_tensor(ph["hL"][:, i % 3, :], ph["h32"][:, i % 2, :],
                                          ph["hH"][:, i % 3, :].bitcast(F32), ALU.subtract).then_inc(ph["h_low"], 1)
                    dve.wait_ge(ph["down"], FT)
                    for t in range(TT):
                        if t >= 2:
                            dve.wait_ge(ph["x_out"], t - 1)
                        dve.tensor_tensor(ph["y"][:, t % 2, :], bank[4 + t][:, :], row[:, 1, :], ALU.mult)\
                            .then_inc(ph["scaled"], 1)
                        dve.wait_ge(ph["scaled"], t + 1)
                        dve.tensor_tensor(X[:, t, :], X[:, t, :], ph["y"][:, t % 2, :], ALU.add)\
                            .then_inc(ph["x_out"], 1)

        def mixer():
            sems = LN_SEMS + ["nt_act", "nt_dve", "in_mm", "gate_mm", "pads", "proj", "conv", "convd", "sig", "act_x",
                              "gated", "dt_w", "dt_mm", "e_chain", "relu", "dt", "decay", "drive", "scan", "skip", "y",
                              "comb", "out_mm", "x_out"]
            bufs = dict(LN_BUFS)
            bufs |= {"nT": ([P, KT, SEQ], F32), "pj": ([P, 2, SEQ + DCONV - 1], F32), "cv": ([P, 2, SEQ], F32),
                     "sg": ([P, 2, SEQ], F32), "Xs": ([P, MT, SEQ], F32), "gate": ([P, MT, SEQ], F32),
                     "ea": ([P, 2, SEQ], F32), "el": ([P, 2, SEQ], F32), "rl": ([P, 2, SEQ], F32),
                     "dtv": ([P, 2, SEQ], F32), "dec": ([P, 2, SEQ], F32), "drv": ([P, 2, SEQ], F32),
                     "st": ([P, 2, SEQ], F32), "sk": ([P, 2, SEQ], F32), "cb": ([P, 2, SEQ], F32),
                     "dtw": ([P, MT, P], F32)}
            with phase("mix", sems, bufs) as (ph, block):
                @block.tensor
                def _(pe):
                    layernorm_turn(pe, ph)
                    pe.wait_ge(ph["nt_act"], 2)
                    pe.wait_ge(ph["nt_dve"], 2)
                    for j in range(MT):
                        for o, (w, done, used) in enumerate(((mix_in, ph["in_mm"], ph["proj"]),
                                                             (mix_gate, ph["gate_mm"], ph["gated"]))):
                            if j >= 2:
                                pe.wait_ge(used, j - 1)
                            for k in range(KT):
                                last = pe.matmul(bank[2 * o + j % 2][:, :], w[:, k, j * P:(j + 1) * P],
                                                 ph["nT"][:, k, :], start=(k == 0), stop=(k == KT - 1))
                            last.then_inc(done, 1)

                    def project_out(j):
                        pe.wait_ge(ph["comb"], j + 1)
                        for t in range(TT):
                            last = pe.matmul(bank[4 + t][:, :], ph["cb"][:, j % 2, t * P:(t + 1) * P],
                                             mix_out[:, j, :], start=(j == 0), stop=(j == MT - 1))
                        last.then_inc(ph["out_mm"], 1)

                    pe.wait_ge(ph["dt_w"], MT)
                    for j in range(MT):
                        pe.wait_ge(ph["act_x"], j + 1)
                        if j < 2:
                            pe.wait_ge(ph["proj"], MT)
                        else:
                            pe.wait_ge(ph["relu"], j - 1)
                        pe.matmul(bank[j % 2][:, :], ph["dtw"][:, j, :], ph["Xs"][:, j, :], start=True, stop=True)\
                            .then_inc(ph["dt_mm"], 1)
                        if j >= 1:
                            project_out(j - 1)
                    project_out(MT - 1)

                @block.scalar
                def _(act):
                    for k in (0, 2):
                        act.wait_ge(ph["turned"], k + 1)
                        act.activation(ph["nT"][:, k, :], bank[k][:, :], ACT.Copy).then_inc(ph["nt_act"], 1)

                    def silu_gate(j):
                        act.wait_ge(ph["convd"], j + 1)
                        if j >= 2:
                            act.wait_ge(ph["act_x"], j - 1)
                        act.activation(ph["sg"][:, j % 2, :], ph["cv"][:, j % 2, :], ACT.Sigmoid).then_inc(ph["sig"], 1)

                    for j in range(MT):
                        act.wait_ge(ph["in_mm"], j + 1)
                        act.wait_ge(ph["pads"], 2)
                        if j >= 2:
                            act.wait_ge(ph["convd"], j - 1)
                        act.activation(ph["pj"][:, j % 2, DCONV - 1:], bank[j % 2][:, :], ACT.Copy)\
                            .then_inc(ph["proj"], 1)
                        act.wait_ge(ph["gate_mm"], j + 1)
                        act.activation(ph["gate"][:, j, :], bank[2 + j % 2][:, :], ACT.Sigmoid)\
                            .then_inc(ph["gated"], 1)
                        if j >= 1:
                            silu_gate(j - 1)
                    silu_gate(MT - 1)
                    act.preload_act_table_set("natural_log_exp_and_others")
                    for j in range(MT):
                        s = j % 2
                        act.wait_ge(ph["dt_mm"], j + 1)
                        act.activation(ph["ea"][:, s, :], bank[s][:, :], ACT.Abs, bias=c("dt_b", j))\
                            .then_inc(ph["e_chain"], 1)
                        act.wait_ge(ph["e_chain"], 2 * j + 1)
                        act.activation(ph["ea"][:, s, :], ph["ea"][:, s, :], ACT.Exp, scale=-1.0).then_inc(ph["e_chain"], 1)
                        act.wait_ge(ph["e_chain"], 2 * j + 2)
                        if j >= 2:
                            act.wait_ge(ph["dt"], j - 1)
                        act.activation(ph["el"][:, s, :], ph["ea"][:, s, :], ACT.Ln, bias=1.0).then_inc(ph["conv"], 1)
                        act.wait_ge(ph["dt"], j + 1)
                        if j >= 2:
                            act.wait_ge(ph["scan"], j - 1)
                        act.activation(ph["dec"][:, s, :], ph["dtv"][:, s, :], ACT.Exp, scale=negA[:, j:j + 1])\
                            .then_inc(ph["decay"], 1)

                @block.vector
                def _(dve):
                    layernorm_vector(dve, ph)
                    for k in (1, 3):
                        dve.wait_ge(ph["turned"], k + 1)
                        dve.tensor_copy(ph["nT"][:, k, :], bank[k][:, :]).then_inc(ph["nt_dve"], 1)
                    n = 0
                    for j in range(MT):
                        s = j % 2
                        dve.wait_ge(ph["proj"], j + 1)
                        if j >= 2:
                            dve.wait_ge(ph["act_x"], j - 1)
                        cv = ph["cv"][:, s, :]
                        w = COLS["conv_w"] + j * DCONV
                        dve.tensor_scalar(cv, ph["pj"][:, s, 0:SEQ], col[:, w:w + 1], c("conv_b", j),
                                          ALU.mult, ALU.add).then_inc(ph["y"], 1)
                        n += 1
                        for k in range(1, DCONV):
                            dve.wait_ge(ph["y"], n)
                            last = dve.scalar_tensor_tensor(out=cv, in0=ph["pj"][:, s, k:k + SEQ],
                                                            scalar=col[:, w + k:w + k + 1], in1=cv,
                                                            op0=ALU.mult, op1=ALU.add)
                            if k < DCONV - 1:
                                last.then_inc(ph["y"], 1)
                                n += 1
                        last.then_inc(ph["convd"], 1)
                    for j in range(MT):
                        s = j % 2
                        dve.wait_ge(ph["e_chain"], 2 * j + 1)
                        if j >= 2:
                            dve.wait_ge(ph["dt"], j - 1)
                        dve.tensor_scalar(ph["rl"][:, s, :], bank[s][:, :], c("dt_b", j), 0.0, ALU.add, ALU.max)\
                            .then_inc(ph["relu"], 1)
                        dve.wait_ge(ph["relu"], j + 1)
                        dve.wait_ge(ph["conv"], j + 1)
                        if j >= 2:
                            dve.wait_ge(ph["decay"], j - 1)
                        dve.tensor_tensor(ph["dtv"][:, s, :], ph["rl"][:, s, :], ph["el"][:, s, :], ALU.add)\
                            .then_inc(ph["dt"], 1)
                        dve.wait_ge(ph["dt"], j + 1)
                        dve.scalar_tensor_tensor(out=ph["drv"][:, s, :], in0=ph["dtv"][:, s, :], scalar=c("Bp", j),
                                                 in1=ph["Xs"][:, j, :], op0=ALU.mult, op1=ALU.mult)\
                            .then_inc(ph["drive"], 1)
                        dve.wait_ge(ph["drive"], j + 1)
                        dve.wait_ge(ph["decay"], j + 1)
                        dve.tensor_tensor_scan(ph["st"][:, s, :], ph["dec"][:, s, :], ph["drv"][:, s, :], 0.0,
                                               ALU.mult, ALU.add).then_inc(ph["scan"], 1)
                        dve.wait_ge(ph["scan"], j + 1)
                        dve.wait_ge(ph["skip"], j + 1)
                        dve.scalar_tensor_tensor(out=ph["st"][:, s, :], in0=ph["st"][:, s, :], scalar=c("Cp", j),
                                                 in1=ph["sk"][:, s, :], op0=ALU.mult, op1=ALU.add)\
                            .then_inc(ph["y"], 1)
                        n += 1
                        dve.wait_ge(ph["y"], n)
                        if j >= 2:
                            dve.wait_ge(ph["out_mm"], j - 1)
                        dve.tensor_tensor(ph["cb"][:, s, :], ph["st"][:, s, :], ph["gate"][:, j, :], ALU.mult)\
                            .then_inc(ph["comb"], 1)
                    dve.wait_ge(ph["out_mm"], MT)
                    for t in range(TT):
                        dve.tensor_tensor(X[:, t, :], bank[4 + t][:, :], X[:, t, :], ALU.add)\
                            .then_inc(ph["x_out"], 1)

                @block.gpsimd
                def _(pool):
                    for s in range(2):
                        pool.memset(ph["pj"][:, s, 0:DCONV - 1], 0.0).then_inc(ph["pads"], 1)
                    for j in range(MT):
                        pool.tensor_scalar(ph["dtw"][:, j, :], hmask[:, :], c("dt_w", j), None, ALU.mult)\
                            .then_inc(ph["dt_w"], 1)
                    for j in range(MT):
                        pool.wait_ge(ph["sig"], j + 1)
                        pool.tensor_tensor(ph["Xs"][:, j, :], ph["cv"][:, j % 2, :], ph["sg"][:, j % 2, :], ALU.mult)\
                            .then_inc(ph["act_x"], 1)
                    pool.wait_ge(ph["act_x"], MT)
                    for j in range(MT):
                        if j >= 2:
                            pool.wait_ge(ph["comb"], j - 1)
                        pool.tensor_scalar(ph["sk"][:, j % 2, :], ph["Xs"][:, j, :], c("Dp", j), None, ALU.mult)\
                            .then_inc(ph["skip"], 1)

        setup()
        with nc.Fori(0, BATCH) as b:
            attention(b)
            ffn("ffn1", load_mix_weights)
            mixer()
            ffn("ffn2", load_att_weights, store_to=b)


def kernel(**inputs):
    import numpy as np
    import concourse.bacc as bacc
    from concourse.bass_utils import run_bass_kernel_spmd

    a = {k: np.asarray(v) for k, v in inputs.items()}
    A, B, C = "L0_attn_a_", "L0_attn_b_", "L0_ffn_"

    def columns(v, width):
        return v.reshape(width, P).T

    def feature_first(w):
        return w.reshape((GROUPS, HG, HD) + w.shape[1:]).swapaxes(1, 2).reshape(w.shape)

    conv_w = a[B + "conv_w"].reshape(MT, P, DCONV).transpose(1, 0, 2).reshape(P, MT * DCONV)
    gates = [a[A + g + "_gate"] for g in ("truth", "balance", "order", "justice", "harmony")]
    cols = np.concatenate(
        [columns(feature_first(a[A + "bq"]), KT), columns(feature_first(a[A + "bk"]), KT),
         columns(a[C + "gate_scale"], FT), columns(a[C + "up_scale"], FT), conv_w,
         columns(a[B + "conv_b"], MT), columns(a[B + "dt_w"], MT),
         columns(np.repeat(a[B + "dt_b"], HDIM), MT)]
        + [columns(a[B + n], MT) for n in ("A_log", "Bp", "Cp", "Dp")]
        + [np.broadcast_to(g, (P, 1)) for g in gates], axis=1)
    rows = np.broadcast_to(np.stack([a[A + "bo"], a[C + "down_scale"], a[A + "bv"]]), (P, 3, DM))
    i = np.arange(P)
    arrays = {
        "x": a[A + "hidden_states"],
        "wq": feature_first(a[A + "Wq"]).T, "wk": feature_first(a[A + "Wk"]).T, "wv": a[A + "Wv"].T, "wo": a[A + "Wo"].T,
        "w_gate": a[C + "gate_w"], "w_up": a[C + "up_w"], "w_down": a[C + "down_w"],
        "w_in": a[B + "in_proj_w"].T, "w_mg": a[B + "gate_proj_w"].T, "w_out": a[B + "out_proj_w"].T,
        "cols": cols, "rows": rows,
        "identity": np.eye(P, dtype=np.float32),
        "head_mask": (i[:, None] // HDIM == i[None, :] // HDIM).astype(np.float32),
        "group_mask": (i[:, None] % HG == np.arange(HG)[None, :]).astype(np.float32),
        "key_pos": np.tile((np.arange(SEQ) * ORDER_STEP).astype(np.float32), (ROW_TERMS, 1)),
    }
    arrays = {k: np.ascontiguousarray(v) for k, v in arrays.items()}
    nc = bacc.Bacc("TRN2", target_bir_lowering=False, num_devices=1)
    args = [nc.dram_tensor(k, v.shape, mybir.dt.from_np(v.dtype), kind="ExternalInput").ap()
            for k, v in arrays.items()]
    out = nc.dram_tensor("out", (BATCH, SEQ, DM), F32, kind="ExternalOutput").ap()
    hybrid_layers(nc, *args, out)
    r = run_bass_kernel_spmd(nc, [arrays], core_ids=[0])
    return r.results[0]["out"]
```

```python
from contextlib import ExitStack, contextmanager
import math

import concourse.bass as bass
from concourse import mybir

F32 = mybir.dt.float32
F32R = mybir.dt.float32r
I32 = mybir.dt.int32
FP8 = mybir.dt.float8e4
BF16 = mybir.dt.bfloat16
ALU = mybir.AluOpType
ACT = mybir.ActivationFunctionType
AX = mybir.AxisListType.X

P = 128
BATCH, SEQ, DM = 4, 512, 512
HEADS, HD = 16, 32
TT = SEQ // P
KT = DM // P
HG = P // HD
GROUPS = HEADS // HG
GT = HG * TT
NS = HEADS * TT
FF = 1536
FT = FF // P
INNER, HDIM, DCONV = 1024, 64, 4
MT = INNER // P
EPS = 1e-5
ORDER_STEP = 0.05 / SEQ

KSTK = 3 * HD
ROW_R = KSTK
ROW_O = KSTK + 2
KALL = KSTK + 4
NPT = 4
ROW_TERMS = 64 + 3 * HG
LAG = 24

COLS = {}
_at = 0
for _n, _w in (("bq", KT), ("bk", KT), ("gate_scale", FT), ("up_scale", FT), ("conv_w", MT * DCONV),
               ("conv_b", MT), ("dt_w", MT), ("dt_b", MT), ("A_log", MT), ("Bp", MT), ("Cp", MT),
               ("Dp", MT), ("gates", 5)):
    COLS[_n] = _at
    _at += _w
NCOL = _at


def hybrid_layers(nc, x, wq, wk, wv, wo, w_gate, w_up, w_down, w_in, w_mg, w_out, cols, rows,
                  identity, head_mask, group_mask, key_pos, out):
    ctx = ExitStack()
    with ctx:
        def sb(name, shape, dt=F32, c=ctx):
            return c.enter_context(nc.sbuf_tensor(name, shape, dt))

        bank = [ctx.enter_context(nc.psum_tensor(f"bank{i}", [P, 512], F32)) for i in range(8)]

        X = sb("X", [P, TT, DM])
        ffnw = sb("ffnw", [P, FT, 3 * 512], BF16)
        wreg = sb("wreg", [P, 3 * KT * INNER])
        col = sb("col", [P, NCOL])
        row = sb("row", [P, 3, 512])
        ident = sb("ident", [P, P])
        hmask = sb("hmask", [P, P])
        gmask = sb("gmask", [P, HG])
        negA = sb("negA", [P, MT])
        bc = sb("bc", [P, MT])
        bn = sb("bn", [P, TT, 6])
        mv = sb("mv", [P, TT, 2])
        ln_v = sb("ln_v", [P, TT])
        ln_r = sb("ln_r", [P, TT])
        eps = sb("eps", [P, 1])
        coef = sb("coef", [P, 8])
        ones32 = sb("ones32", [P, HD])
        row_terms = sb("row_terms", [ROW_TERMS, SEQ], F32R)
        ones_row, order_h, order_l = (row_terms[q:q + 3 * HG, :] for q in (0, 32, 64))
        C_T, C_B, C_O, C_J, C_H, C_A, C_RA = range(7)

        att_w = wreg[:, 0:4 * KT * DM].rearrange("p (m k n) -> p m k n", m=4, k=KT)
        att_tail = wreg[:, 4 * KT * DM:]
        nT_att = att_tail[:, 0:KT * SEQ].rearrange("p (k n) -> p k n", k=KT)
        V = att_tail[:, KT * SEQ:].rearrange("p (t n) -> p t n", t=TT)
        mix_in = wreg[:, 0:KT * INNER].rearrange("p (k n) -> p k n", k=KT)
        mix_gate = wreg[:, KT * INNER:2 * KT * INNER].rearrange("p (k n) -> p k n", k=KT)
        mix_out = wreg[:, 2 * KT * INNER:].rearrange("p (j n) -> p j n", j=MT)

        def c(name, j=0):
            return col[:, COLS[name] + j:COLS[name] + j + 1]

        def load_att_weights(sp, done):
            for m, w in enumerate((wq, wk, wv, wo)):
                sp.dma_start(att_w[:, m], w.rearrange("(k p) n -> p k n", p=P)).then_inc(done, 16)

        def load_mix_weights(sp, done):
            for dst, w in ((mix_in, w_in), (mix_gate, w_mg), (mix_out, w_out)):
                sp.dma_start(dst, w.rearrange("(k p) n -> p k n", p=P)).then_inc(done, 16)

        def move(eng, dst, src, done):
            eng.dma_start(dst.bitcast(F32), src.bitcast(F32)).then_inc(done, 16)

        @contextmanager
        def phase(name, sems, buffers):
            with ExitStack() as stack:
                ph = {n: stack.enter_context(nc.semaphore(f"{name}_{n}")) for n in sems}
                ph.update({n: sb(f"{name}_{n}", shape, dt, stack) for n, (shape, dt) in buffers.items()})
                with nc.Block() as block:
                    yield ph, block
                for i, n in enumerate(sems):
                    (nc.sync, nc.scalar, nc.vector, nc.gpsimd)[i % 4].sem_clear(ph[n])
                nc.all_engine_barrier()

        LN_SEMS = ["x_stats", "moments", "rstd", "normed"]

        def token_stats(dve, ph, t, src):
            dve.bn_stats(bn[:, t, :], src[:, t, :]).then_inc(ph["x_stats"], 1)
            dve.wait_ge(ph["x_stats"], t + 1)
            dve.bn_aggr(mv[:, t, :], bn[:, t, :]).then_inc(ph["moments"], 1)

        def normalise(dve, ph, t, src):
            dve.wait_ge(ph["rstd"], 2 * (t + 1))
            dve.tensor_scalar(ph["N"][:, t, :], src[:, t, :], mv[:, t, 0:1], ln_r[:, t:t + 1],
                              ALU.subtract, ALU.mult).then_inc(ph["normed"], 1)

        def layernorm_vector(dve, ph, finish):
            for t in range(TT):
                finish(t)
                token_stats(dve, ph, t, X)
                if t >= 1:
                    normalise(dve, ph, t - 1, X)
            normalise(dve, ph, TT - 1, X)

        def layernorm_scalar(act, ph):
            act.preload_act_table_set("natural_log_exp_and_others")
            for t in range(TT):
                act.wait_ge(ph["moments"], t + 1)
                act.activation(ln_v[:, t:t + 1], mv[:, t, 1:2], ACT.Ln, bias=eps[:, :]).then_inc(ph["rstd"], 1)
                act.wait_ge(ph["rstd"], 2 * t + 1)
                act.activation(ln_r[:, t:t + 1], ln_v[:, t:t + 1], ACT.Exp, scale=-0.5).then_inc(ph["rstd"], 1)

        def layernorm_turn(pe, ph, to):
            for t in range(TT):
                pe.wait_ge(ph["normed"], t + 1)
                for k in range(KT):
                    pe.transpose(bank[to + k][:, t * P:(t + 1) * P], ph["N"][:, t, k * P:(k + 1) * P], ident[:, :])

        def setup():
            sems = LN_SEMS + ["loaded", "x_in", "staged0", "staged1", "weights", "chain", "ones", "gate_exp", "clipped", "bias", "halved", "low_far", "high_far",
                    "far_ready", "tile_done"]
            bufs = {"N": ([P, TT, DM], F32), "stage": ([P, 2, 3 * 512], F32), "body": ([P, 2, 3 * 512], FP8), "half": ([P, 2, 3 * 512], FP8),
                    "above": ([P, 2, 3 * 512], BF16), "below": ([P, 2, 3 * 512], BF16),
                    "far": ([P, 2, 3 * 512], F32), "m64": ([P, 1], F32), "sg": ([P, 5], F32),
                    "pos": ([ROW_TERMS, SEQ], F32), "o32": ([ROW_TERMS, SEQ], F32), "one": ([3 * HG, SEQ], F32)}
            with phase("setup", sems, bufs) as (ph, block):
                staged = (ph["staged0"], ph["staged1"])

                @block.sync
                def _(sp):
                    for dst, src in ((col, cols), (row, rows), (ident, identity), (hmask, head_mask),
                                     (gmask, group_mask), (ph["pos"], key_pos)):
                        sp.dma_start(dst[:], src).then_inc(ph["loaded"], 16)
                    for t in range(TT):
                        sp.dma_start(X[:, t, :], x[0, t * P:(t + 1) * P, :]).then_inc(ph["x_in"], 16)
                    for i in range(FT):
                        if i >= 2:
                            sp.wait_ge(ph["clipped"], i - 1)
                            sp.wait_ge(ph["halved"], i - 1)
                        f = slice(i * P, (i + 1) * P)
                        st = ph["stage"][:, i % 2].rearrange("p (m k n) -> p m k n", m=3, k=KT)
                        for m, w in enumerate((w_gate, w_up)):
                            sp.dma_start(st[:, m], w.rearrange("(k p) n -> p k n", p=P)[:, :, f])\
                                .then_inc(staged[i % 2], 16)
                        sp.dma_start(ph["stage"][:, i % 2, 1024:1536], w_down[f, :]).then_inc(staged[i % 2], 16)
                    load_att_weights(sp, ph["weights"])
                    sp.wait_ge(ph["weights"], 16 * 4)

                @block.vector
                def _(dve):
                    n = 0

                    def chained(ins):
                        nonlocal n
                        n += 1
                        ins.then_inc(ph["chain"], 1)
                        dve.wait_ge(ph["chain"], n)

                    def join(i):
                        dve.wait_ge(ph["clipped"], i + 1)
                        dve.wait_ge(ph["far_ready"], i + 1)
                        dve.scalar_tensor_tensor(out=ffnw[:, i, :], in0=ph["far"][:, i % 2, :], scalar=2.0,
                                                 in1=ph["body"][:, i % 2, :], op0=ALU.mult, op1=ALU.add)\
                            .then_inc(ph["tile_done"], 1)

                    chained(dve.memset(ones32[:, :], 1.0))
                    chained(dve.memset(eps[:, :], EPS))
                    chained(dve.memset(ph["one"][:, :], 1.0))
                    dve.wait_ge(ph["loaded"], 16 * 6)
                    b_, c_ = COLS["Bp"], COLS["Cp"]
                    chained(dve.tensor_tensor(bc[:, :], col[:, b_:b_ + MT], col[:, c_:c_ + MT], ALU.mult))
                    dve.wait_ge(ph["gate_exp"], 1)
                    chained(dve.tensor_scalar(ph["sg"][:, :], ph["sg"][:, :], 1.0, None, ALU.add))
                    chained(dve.reciprocal(ph["sg"][:, :], ph["sg"][:, :]))
                    for k, (g, f) in {C_T: (0, -0.01), C_B: (1, 0.1 / math.log(SEQ)), C_O: (2, 1.0),
                                      C_J: (3, 0.1), C_H: (4, -0.1 / (SEQ - 1))}.items():
                        chained(dve.tensor_scalar(coef[:, k:k + 1], ph["sg"][:, g:g + 1], f, None, ALU.mult))
                    chained(dve.tensor_scalar(coef[:, C_A:C_A + 1], coef[:, C_J:C_J + 1], -1.0, 1.0,
                                              ALU.mult, ALU.add))
                    chained(dve.reciprocal(coef[:, C_RA:C_RA + 1], coef[:, C_A:C_A + 1]))
                    chained(dve.tensor_scalar(ph["o32"][:, :], ph["pos"][:, :], coef[0:ROW_TERMS, C_O:C_O + 1],
                                              coef[0:ROW_TERMS, C_RA:C_RA + 1], ALU.mult, ALU.mult))
                    chained(dve.tensor_copy(row_terms[:, :], ph["o32"][:, :]))
                    chained(dve.tensor_tensor(order_l, ph["o32"][64:ROW_TERMS, :], order_l.bitcast(F32),
                                              ALU.subtract))
                    chained(dve.tensor_copy(ones_row, ph["one"][:, :]))
                    dve.wait_ge(ph["gate_exp"], 2)
                    chained(dve.tensor_scalar(negA[:, :], negA[:, :], -1.0, None, ALU.mult))
                    for i in range(FT):
                        dve.wait_ge(staged[i % 2], 48 * (i // 2 + 1))
                        if i >= 2:
                            dve.wait_ge(ph["tile_done"], i - 1)
                        dve.tensor_scalar(ph["body"][:, i % 2, :], ph["stage"][:, i % 2, :], 128.0, -128.0,
                                          ALU.min, ALU.max, saturate=False).then_inc(ph["clipped"], 1)
                        dve.wait_ge(ph["halved"], i + 1)
                        if i >= 2:
                            dve.wait_ge(ph["far_ready"], i - 1)
                        dve.tensor_scalar(ph["below"][:, i % 2, :], ph["half"][:, i % 2, :], 64.0, 0.0,
                                          ALU.add, ALU.min).then_inc(ph["low_far"], 1)
                        if i >= 1:
                            join(i - 1)
                    join(FT - 1)
                    dve.wait_ge(ph["x_in"], 16 * TT)
                    layernorm_vector(dve, ph, lambda t: None)

                @block.tensor
                def _(pe):
                    pe.wait_ge(ph["loaded"], 16 * 6)
                    layernorm_turn(pe, ph, 0)

                @block.scalar
                def _(act):
                    act.wait_ge(ph["loaded"], 16 * 6)
                    g = COLS["gates"]
                    act.activation(ph["sg"][:, :], col[:, g:g + 5], ACT.Exp, scale=-1.0).then_inc(ph["gate_exp"], 1)
                    a = COLS["A_log"]
                    act.activation(negA[:, :], col[:, a:a + MT], ACT.Exp).then_inc(ph["gate_exp"], 1)
                    act.wait_ge(ph["bias"], 1)
                    for i in range(FT):
                        act.wait_ge(staged[i % 2], 48 * (i // 2 + 1))
                        if i >= 2:
                            act.wait_ge(ph["low_far"], i - 1)
                        act.activation(ph["half"][:, i % 2, :], ph["stage"][:, i % 2, :], ACT.Copy, scale=0.5,
                                       saturate=False).then_inc(ph["halved"], 1)
                        act.wait_ge(ph["halved"], i + 1)
                        if i >= 2:
                            act.wait_ge(ph["far_ready"], i - 1)
                        act.activation(ph["above"][:, i % 2, :], ph["half"][:, i % 2, :], ACT.Relu,
                                       bias=ph["m64"][:, :]).then_inc(ph["high_far"], 1)
                    layernorm_scalar(act, ph)

                @block.gpsimd
                def _(pool):
                    pool.memset(ph["m64"][:, :], -64.0).then_inc(ph["bias"], 1)
                    for i in range(FT):
                        pool.wait_ge(ph["high_far"], i + 1)
                        pool.wait_ge(ph["low_far"], i + 1)
                        if i >= 2:
                            pool.wait_ge(ph["tile_done"], i - 1)
                        pool.tensor_tensor(ph["far"][:, i % 2, :], ph["above"][:, i % 2, :],
                                           ph["below"][:, i % 2, :], ALU.add).then_inc(ph["far_ready"], 1)

        def attention():
            order = ["k0", "q0", "q1", "s0"] + ["k1", "v0", "v1", "s1", "v2", "q2", "v3"]
            for g in range(1, GROUPS + 1):
                if g + 1 < GROUPS:
                    order += [f"k{g + 1}"]
                if g >= 1:
                    order += [f"r{g - 1}"]
                if g + 1 < GROUPS:
                    order += [f"s{g + 1}"]
                if g + 2 < GROUPS:
                    order += [f"q{g + 2}"]
            order += [f"o{t}" for t in range(TT)]
            DIFF, PROJ, PROB, OUT, SUM = 3, 4, 5, 6, 7
            place = {"q0": 4, "k0": 6, "s0": 7, "v0": 5, "v1": 6, "v2": 7, "v3": 5,
                     "o0": 0, "o1": 1, "o2": 2, "o3": 3}
            I_K, I_R, I_S, I_Q = 0, 4, 7, 12

            def at(name):
                return bank[place.get(name, PROJ)]

            def score_bank(n):
                return bank[n % 3]

            def act_differs(n):
                return n < LAG or n % 2 == 0

            def differed(eng, n):
                on_act = sum(act_differs(j) for j in range(n))
                if on_act:
                    eng.wait_ge(ph["diff_act"], on_act)
                if n > on_act:
                    eng.wait_ge(ph["diff_dve"], n - on_act)

            two, three = NS + 1 - LAG, NS + I_R + 2 - LAG

            def prob_bank(m):
                return bank[PROB if m < two or m % 2 == 0 else DIFF if m < three else PROJ]

            sems = LN_SEMS + ["nt_act", "nt_dve", "filled", "v_ready",
                              "q_ready", "k_ready", "k2_ready", "dk_ready", "mean_w", "q_parts", "k_parts", "d_parts",
                              "const_rows", "stk_qk0", "stk_qk1", "stk_d0", "stk_d1", "score", "maxed", "exped", "ent", "diff", "diff_act",
                              "diff_dve", "prob_mm", "prob", "pv", "scaled", "chain", "stat_read", "lns",
                              "rz_ready", "shift", "shift_h", "shift_l", "shift_rows", "xb", "x_out"]
            bufs = {"OT": ([P, GROUPS, SEQ], F32), "k32": ([P, SEQ], F32), "tmp": ([P, 6, SEQ], F32R), "Qs": ([P, 3, HG, SEQ], F32R),
                     "Ks": ([P, 3, HG, SEQ], F32R), "Ds": ([KSTK, 2, HG, SEQ], F32R), "E": ([P, 2, SEQ], F32),
                     "PT": ([P, NPT, SEQ], F32), "rz": ([P, SEQ], F32), "lnz": ([P, SEQ], F32),
                     "nmax": ([P, NS], F32), "Z": ([P, NS], F32), "U": ([P, NS], F32), "Ab": ([P, NS], F32),
                     "stat": ([P, GROUPS, 2, TT, HG], F32), "ksum": ([P, GROUPS], F32),
                     "meanw": ([P, GROUPS, HG], F32), "w": ([P, 6, GT], F32), "r": ([P, GT], F32),
                     "rh": ([GT, P], F32R), "rl": ([GT, P], F32R)}
            with phase("att", sems, bufs) as (ph, block):
                OT = ph["OT"]
                q32, dk, k2 = OT[:, 1, :], OT[:, 2, :], OT[:, 3, :]
                QH, QL, KH, KL, DH, DL = range(6)
                ph["N"] = ph["PT"]

                def stacked(eng, g, names="qk d"):
                    if "qk" in names:
                        eng.wait_ge(ph[f"stk_qk{g % 2}"], 16 * 6 * (g // 2 + 1))
                    if "d" in names:
                        eng.wait_ge(ph[f"stk_d{g % 2}"], 16 * 3 * (g // 2 + 1))

                def filled(eng, name):
                    eng.wait_ge(ph["filled"], order.index(name) + 1)

                @block.sync
                def _(sp):
                    def const_rows():
                        for dst, row0, src in (("Ks", ROW_R, ones_row), ("Ks", ROW_R + 1, ones_row),
                                               ("Ks", ROW_O, order_h), ("Ks", ROW_O + 1, order_l),
                                               ("Qs", ROW_O, ones_row), ("Qs", ROW_O + 1, ones_row)):
                            move(sp, ph[dst][row0:row0 + 1], src, ph["const_rows"])

                    def stack_up(g):
                        if g >= 2:
                            sp.wait_ge(ph["diff"], GT * (g - 1))
                        if g >= 3:
                            sp.wait_ge(ph["prob_mm"], GT * (g - 2))
                        q = (ph["Qs"][:, g % 3], (QH, QH, QL), ph["q_parts"], "qk")
                        k = (ph["Ks"][:, g % 3], (KH, KL, KH), ph["k_parts"], "qk")
                        d = (ph["Ds"][:, g % 2], (DH, DL, DH), ph["d_parts"], "d")
                        for dst, parts, split, name in (k, q, d) if g == 0 else (q, k, d):
                            sp.wait_ge(split, 2 * (g + 1))
                            for i, part in enumerate(parts):
                                move(sp, dst[HD * i:HD * (i + 1)], ph["tmp"][:, part, :], ph[f"stk_{name}{g % 2}"])

                    def shift_rows(g):
                        sp.wait_ge(ph["shift_h"], g + 1)
                        move(sp, ph["Qs"][ROW_R:ROW_R + 1, g % 3], ph["rh"][:, :], ph["shift_rows"])
                        sp.wait_ge(ph["shift_l"], g + 1)
                        move(sp, ph["Qs"][ROW_R + 1:ROW_R + 2, g % 3], ph["rl"][:, :], ph["shift_rows"])

                    stack_up(0)
                    const_rows()
                    stack_up(1)
                    for g in range(GROUPS):
                        shift_rows(g)
                        if g + 2 < GROUPS:
                            stack_up(g + 2)
                    sp.wait_ge(ph["shift_rows"], 32 * GROUPS)

                @block.tensor
                def _(pe):

                    def project(g, name, m, ks=range(KT)):
                        for k in ks:
                            if name == "k" and g == 0:
                                pe.wait_ge(ph["nt_dve"] if k % 2 else ph["nt_act"], k // 2 + 1)
                            last = pe.matmul(at(f"{name}{g}")[:, :], att_w[:, m, k, g * P:(g + 1) * P],
                                             nT_att[:, k, :], start=(k == 0), stop=(k == KT - 1))
                        if k == KT - 1:
                            last.then_inc(ph["filled"], 1)

                    def key_stats(g, ts):
                        pe.wait_ge(ph["k2_ready"], g + 1)
                        pe.wait_ge(ph["q_ready"], g + 1)
                        pe.wait_ge(ph["mean_w"], g + 1)
                        to = at(f"s{g}")
                        for t in ts:
                            pe.matmul(to[:, HG * t:HG * (t + 1)], k2[:, t * P:(t + 1) * P], gmask[:, :],
                                      start=True, stop=True)
                            last = pe.matmul(to[:, GT + HG * t:GT + HG * (t + 1)], q32[:, t * P:(t + 1) * P],
                                             ph["meanw"][:, g, :], start=True, stop=True)
                        if t == TT - 1:
                            last.then_inc(ph["filled"], 1)

                    def score(n):
                        g, i = divmod(n, GT)
                        h, t = divmod(i, TT)
                        if i == 0:
                            stacked(pe, g, "qk")
                        if n >= 3:
                            pe.wait_ge(ph["ent"], n - 2)
                        pe.matmul(score_bank(n)[:, :], ph["Qs"][0:KSTK, g % 3, h, t * P:(t + 1) * P],
                                  ph["Ks"][0:KSTK, g % 3, h, :], start=True, stop=True).then_inc(ph["score"], 1)

                    def difference(n):
                        g, i = divmod(n, GT)
                        h, t = divmod(i, TT)
                        if i == 0:
                            stacked(pe, g, "d")
                        if n >= 1:
                            differed(pe, n)
                        pe.matmul(bank[DIFF][:, :], ph["Qs"][0:KSTK, g % 3, h, t * P:(t + 1) * P],
                                  ph["Ds"][:, g % 2, h, :], start=True, stop=True).then_inc(ph["diff"], 1)

                    def probability(m):
                        gm, im = divmod(m, GT)
                        h, k = divmod(im, TT)
                        if m == 0:
                            pe.wait_ge(ph["const_rows"], 16 * 6)
                            pe.wait_ge(ph["v_ready"], TT)
                        if im == 0:
                            pe.wait_ge(ph["shift_rows"], 32 * (gm + 1))
                        if m == two:
                            differed(pe, NS)
                        if m == three + 1:
                            pe.wait_ge(ph["shift_l"], GROUPS)
                        if m >= 1:
                            pe.wait_ge(ph["prob"], m - 1 if m > two else m)
                        pe.matmul(prob_bank(m)[:, :], ph["Ks"][0:KALL, gm % 3, h, k * P:(k + 1) * P],
                                  ph["Qs"][0:KALL, gm % 3, h, :], start=True, stop=True).then_inc(ph["prob_mm"], 1)

                    def weigh(m):
                        gm, im = divmod(m, GT)
                        h, k = divmod(im, TT)
                        pe.wait_ge(ph["prob"], m + 1)
                        if im == 0 and gm >= 1:
                            pe.wait_ge(ph["scaled"], gm)
                        hs = slice(HD * h, HD * (h + 1))
                        vs = slice((gm * HG + h) * HD, (gm * HG + h + 1) * HD)
                        pe.matmul(bank[OUT][hs, :], V[:, k, vs], ph["PT"][:, m % NPT, :], start=(k == 0),
                                  stop=(k == TT - 1), tile_position=(0, HD * h))
                        hs = (HD * h + P // 2) % P
                        pe.matmul(bank[SUM][hs:hs + HD, :], ones32[:, :], ph["PT"][:, m % NPT, :], start=(k == 0),
                                  stop=(k == TT - 1), tile_position=(0, hs)).then_inc(ph["pv"], 1)

                    def output(t, g):
                        pe.wait_ge(ph["scaled"], g + 1)
                        last = pe.matmul(at(f"o{t}")[:, :], OT[:, g, t * P:(t + 1) * P],
                                         att_w[:, 3, g, :], start=(g == 0), stop=(g == GROUPS - 1))
                        if g == GROUPS - 1:
                            last.then_inc(ph["filled"], 1)

                    def value(t, k):
                        if k == 0 and t == TT - 1:
                            pe.wait_ge(ph["v_ready"], 1)
                        elif k == 0 and t == 2:
                            pe.wait_ge(ph["stat_read"], 1)
                        last = pe.matmul(at(f"v{t}")[:, :], nT_att[:, k, t * P:(t + 1) * P],
                                         att_w[:, 2, k, :], start=(k == 0), stop=(k == KT - 1))
                        if k == KT - 1:
                            last.then_inc(ph["filled"], 1)

                    project(0, "k", 1)
                    project(0, "q", 0)
                    pe.wait_ge(ph["q_ready"], 1)
                    project(1, "q", 0)
                    key_stats(0, range(TT))
                    score(0)
                    score(1)
                    for n in range(NS + LAG + 1):
                        g, i = divmod(n, GT)
                        m = n - LAG
                        if 0 <= m < NS:
                            probability(m)
                        if n + 2 < NS:
                            score(n + 2)
                        if m >= GT and (m - 1) % GT == NPT - 2:
                            for late in range(m - NPT + 1, m - 1):
                                weigh(late)
                        if m >= 1 and (m <= GT or (m - 1) % GT >= NPT - 2):
                            weigh(m - 1)
                        if I_K <= i < I_K + KT and g + 1 < GROUPS:
                            if i == I_K:
                                pe.wait_ge(ph["q_ready"], g + 2)
                            project(g + 1, "k", 1, [i - I_K])
                        if i == I_R and 1 <= g <= GROUPS:
                            pe.wait_ge(ph["shift"], g)
                            if g + 1 < GROUPS:
                                pe.wait_ge(ph["k_ready"], g + 2)
                            pe.transpose(at(f"r{g - 1}")[0:GT, 0:P], ph["r"][:, :], ident[:, :])\
                                .then_inc(ph["filled"], 1)
                        if I_S <= i < I_S + 2 and g + 1 < GROUPS:
                            if g >= 1:
                                pe.wait_ge(ph["shift_l"], g)
                            key_stats(g + 1, range(2 * (i - I_S), 2 * (i - I_S + 1)))
                        if I_Q <= i < I_Q + KT and g + 2 < GROUPS:
                            if i == I_Q:
                                pe.wait_ge(ph["stat_read"], g + 2)
                            project(g + 2, "q", 0, [i - I_Q])
                        if g == 0:
                            value(*divmod(i, KT))
                        if n < NS:
                            difference(n)
                        e = n - (NS + 1)
                        if e == 0:
                            pe.wait_ge(ph["ent"], NS)
                        if 0 <= e < 2 * TT:
                            output(e // 2, e % 2)
                        e = m - (NS - GT + 4)
                        if 0 <= e < TT:
                            output(e, 2)
                    for t in range(TT):
                        output(t, GROUPS - 1)
                    layernorm_turn(pe, ph, 4)

                @block.scalar
                def _(act):
                    act.preload_act_table_set("natural_log_exp_and_others")
                    for k in (0, 2):
                        act.activation(nT_att[:, k, :], bank[k][:, :], ACT.Copy).then_inc(ph["nt_act"], 1)

                    def key(g):
                        filled(act, f"k{g}")
                        if g >= 1:
                            act.wait_ge(ph["k_parts"], 2 * g)
                            act.wait_ge(ph["k2_ready"], g)
                            act.wait_ge(ph["dk_ready"], g)
                        act.activation(ph["k32"][:, :], at(f"k{g}")[:, :], ACT.Identity, bias=c("bk", g),
                                       accum_out=ph["ksum"][:, g:g + 1]).then_inc(ph["k_ready"], 1)

                    key(0)
                    for n in range(NS + LAG + 1):
                        g, i = divmod(n, GT)
                        if i == I_K + KT and g + 1 < GROUPS:
                            key(g + 1)
                        if i == I_R + 1 and 1 <= g <= GROUPS:
                            filled(act, f"r{g - 1}")
                            if g >= 2:
                                act.wait_ge(ph["shift_rows"], 32 * (g - 1))
                            act.activation(ph["rh"][:, :], at(f"r{g - 1}")[0:GT, 0:P], ACT.Copy)\
                                .then_inc(ph["shift_h"], 1)
                        if n < NS:
                            act.wait_ge(ph["maxed"], n + 1)
                            if n >= 2:
                                act.wait_ge(ph["ent"], n - 1)
                            act.activation(ph["E"][:, n % 2, :], score_bank(n)[:, :], ACT.Exp,
                                           bias=ph["nmax"][:, n:n + 1], accum_out=ph["Z"][:, n:n + 1])\
                                .then_inc(ph["exped"], 1)
                        if 1 <= n <= NS and act_differs(n - 1):
                            act.wait_ge(ph["diff"], n)
                            act.activation(bank[DIFF][:, :], bank[DIFF][:, :], ACT.Abs,
                                           accum_out=ph["Ab"][:, n - 1:n]).then_inc(ph["diff_act"], 1)
                        if i == 0 and 1 <= g <= GROUPS:
                            s = slice((g - 1) * GT, g * GT)
                            act.wait_ge(ph["exped"], GT * g)
                            act.activation(ph["w"][:, 0, :], ph["Z"][:, s], ACT.Ln).then_inc(ph["lns"], 1)
                            kn = ph["w"][:, 1, :].rearrange("p (h t) -> p t h", h=HG)
                            act.activation(kn, ph["stat"][:, g - 1, 0], ACT.Ln).then_inc(ph["lns"], 1)
                            act.wait_ge(ph["lns"], 3 * g - 1)
                            act.activation(ph["w"][:, 2, :], ph["w"][:, 1, :], ACT.Exp, scale=0.5).then_inc(ph["lns"], 1)
                        m = n - LAG
                        if m >= 1 and m % GT == 0:
                            act.wait_ge(ph["pv"], m)
                            act.activation(ph["lnz"][:, :], bank[SUM][:, :], ACT.Ln).then_inc(ph["rz_ready"], 1)
                            act.wait_ge(ph["rz_ready"], 3 * (m // GT) - 2)
                            if m > GT:
                                act.wait_ge(ph["scaled"], m // GT - 1)
                            for o, z in ((slice(0, 64), slice(64, P)), (slice(64, P), slice(0, 64))):
                                act.activation(ph["rz"][o, :], ph["lnz"][z, :], ACT.Exp, scale=-1.0)\
                                    .then_inc(ph["rz_ready"], 1)
                        if 0 <= m < NS:
                            act.wait_ge(ph["prob_mm"], m + 1)
                            if m >= NPT:
                                act.wait_ge(ph["pv"], m - NPT + 1)
                            act.activation(ph["PT"][:, m % NPT, :], prob_bank(m)[:, :], ACT.Exp,
                                           scale=coef[:, C_A:C_A + 1]).then_inc(ph["prob"], 1)
                    layernorm_scalar(act, ph)

                @block.vector
                def _(dve):
                    for k in (1, 3):
                        dve.tensor_copy(nT_att[:, k, :], bank[k][:, :]).then_inc(ph["nt_dve"], 1)

                    def split(g, full, hi, lo, done):
                        dve.tensor_copy(ph["tmp"][:, hi, :], full).then_inc(done, 1)
                        if g == 0:
                            dve.wait_ge(done, 1)
                            dve.tensor_tensor(ph["tmp"][:, lo, :], full, ph["tmp"][:, hi, :].bitcast(F32),
                                              ALU.subtract).then_inc(done, 1)

                    def query(g):
                        filled(dve, f"q{g}")
                        if g >= 1:
                            dve.wait_ge(ph["q_parts"], 2 * g)
                            filled(dve, f"s{g - 1}")
                        dve.tensor_scalar(q32, at(f"q{g}")[:, :], c("bq", g), 1 / math.sqrt(HD),
                                          ALU.add, ALU.mult).then_inc(ph["q_ready"], 1)
                        dve.wait_ge(ph["q_ready"], g + 1)
                        if g >= 1:
                            stacked(dve, g - 1)
                        split(g, q32, QH, QL, ph["q_parts"])

                    def split_key(g):
                        dve.wait_ge(ph["k_ready"], g + 1)
                        dve.tensor_scalar(ph["meanw"][:, g, :], gmask[:, :], ph["ksum"][:, g:g + 1], 1 / SEQ,
                                          ALU.mult, ALU.mult).then_inc(ph["mean_w"], 1)
                        split(g, ph["k32"][:, :], KH, KL, ph["k_parts"])

                    def split_difference(g):
                        dve.wait_ge(ph["dk_ready"], g + 1)
                        split(g, dk, DH, DL, ph["d_parts"])

                    def stats(g):
                        filled(dve, f"s{g}")
                        src = at(f"s{g}")[:, 0:2 * GT].rearrange("p (m t h) -> p m t h", m=2, t=TT)
                        dve.tensor_scalar(ph["stat"][:, g, 0], src[:, 0], 1e-18, None, ALU.max)\
                            .then_inc(ph["chain"], 1)
                        dve.tensor_copy(ph["stat"][:, g, 1], src[:, 1]).then_inc(ph["stat_read"], 1)

                    split_key(0)
                    split_difference(0)
                    query(0)

                    def value(t):
                        filled(dve, f"v{t}")
                        dve.tensor_tensor(V[:, t, :], at(f"v{t}")[:, :], row[:, 2, :], ALU.add)\
                            .then_inc(ph["v_ready"], 1)

                    stats(0)
                    chain = 1

                    def chained(ins):
                        nonlocal chain
                        chain += 1
                        ins.then_inc(ph["chain"], 1)
                        dve.wait_ge(ph["chain"], chain)

                    def maximum(n):
                        dve.wait_ge(ph["score"], n + 1)
                        dve.tensor_reduce(ph["nmax"][:, n:n + 1], score_bank(n)[:, :], AX, ALU.max, negate=True)\
                            .then_inc(ph["maxed"], 1)

                    def shift_part(g, j):
                        s = slice(g * GT, (g + 1) * GT)
                        w = ph["w"]
                        knorm, ent, acc, top = w[:, 2, :], w[:, 3, :], w[:, 4, :], w[:, 5, :]
                        mean = ph["stat"][:, g, 1].rearrange("p t h -> p h t")
                        acc_ht = acc.rearrange("p (h t) -> p h t", h=HG)

                        def k_(j):
                            return coef[:, j:j + 1]

                        def add(out, x, factor, y, op=ALU.add):
                            return dve.scalar_tensor_tensor(out=out, in0=x, scalar=k_(factor), in1=y,
                                                            op0=ALU.mult, op1=op)

                        nonlocal chain
                        if j == 0:
                            dve.wait_ge(ph["ent"], GT * (g + 1))
                            dve.wait_ge(ph["lns"], 3 * (g + 1))
                            differed(dve, GT * (g + 1))
                        else:
                            dve.wait_ge(ph["chain"], chain)
                        chain += 1
                        if j == 0:
                            done = dve.reciprocal(ent, ph["Z"][:, s])
                        elif j == 1:
                            done = dve.tensor_tensor(ent, ent, ph["U"][:, s], ALU.mult)
                        elif j == 2:
                            done = dve.tensor_tensor(ent, w[:, 0, :], ent, ALU.subtract)
                        elif j == 3:
                            done = dve.tensor_scalar(acc, knorm, k_(C_T), None, ALU.mult)
                        elif j == 4:
                            done = add(acc, ent, C_B, acc)
                        elif j == 5:
                            done = add(acc_ht, mean, C_J, acc_ht)
                        elif j == 6:
                            done = add(acc, ph["Ab"][:, s], C_H, acc)
                        elif j == 7:
                            done = add(top, ph["nmax"][:, s], C_A, acc, ALU.subtract)
                        elif j == 8:
                            done = dve.tensor_tensor(acc, top, acc, ALU.add)
                        else:
                            if g >= 1:
                                dve.wait_ge(ph["shift_h"], g)
                            chain -= 1
                            dve.tensor_scalar(ph["r"][:, :], acc, k_(C_RA), None, ALU.mult).then_inc(ph["shift"], 1)
                            return
                        done.then_inc(ph["chain"], 1)

                    maximum(0)
                    for n in range(NS + LAG + 1):
                        g, i = divmod(n, GT)
                        shifting = 1 <= g <= GROUPS and i < 4
                        if i == 0 and g + 1 < GROUPS:
                            query(g + 1)
                        if n and n <= GT and n % KT == 0:
                            value(n // KT - 1)
                        if n + 1 < NS:
                            maximum(n + 1)
                        if shifting and i > 0:
                            shift_part(g - 1, 3 * i - 2)
                        if 1 <= n <= NS and not act_differs(n - 1):
                            dve.wait_ge(ph["diff"], n)
                            dve.tensor_reduce(ph["Ab"][:, n - 1:n], bank[DIFF][:, :], AX, ALU.add,
                                              apply_absolute_value=True).then_inc(ph["diff_dve"], 1)
                        if shifting and i > 0:
                            shift_part(g - 1, 3 * i - 1)
                        if n < NS:
                            dve.wait_ge(ph["exped"], n + 1)
                            dve.scalar_tensor_tensor(out=ph["E"][:, n % 2, :], in0=score_bank(n)[:, :],
                                                     scalar=ph["nmax"][:, n:n + 1], in1=ph["E"][:, n % 2, :],
                                                     op0=ALU.add, op1=ALU.mult, accum_out=ph["U"][:, n:n + 1])\
                                .then_inc(ph["ent"], 1)
                        if g + 1 < GROUPS:
                            if i == I_K + KT:
                                split_key(g + 1)
                            if i == I_K + KT + 1:
                                split_difference(g + 1)
                            if i == I_S + 2:
                                stats(g + 1)
                                chain += 1
                        if shifting:
                            shift_part(g - 1, 3 * i)
                        if i == I_R + 1 and 1 <= g <= GROUPS:
                            dve.wait_ge(ph["shift_h"], g)
                            if g >= 2:
                                dve.wait_ge(ph["shift_rows"], 32 * (g - 1))
                            dve.tensor_tensor(ph["rl"][:, :], at(f"r{g - 1}")[0:GT, 0:P],
                                              ph["rh"][:, :].bitcast(F32), ALU.subtract).then_inc(ph["shift_l"], 1)
                        m = n - LAG
                        if m >= 1 and m % GT == 0:
                            gm = m // GT - 1
                            dve.wait_ge(ph["pv"], m)
                            dve.wait_ge(ph["rz_ready"], 3 * (gm + 1))
                            dve.tensor_tensor(OT[:, gm, :], bank[OUT][:, :], ph["rz"][:, :], ALU.mult)\
                                .then_inc(ph["scaled"], 1)

                    def finish(t):
                        filled(dve, f"o{t}")
                        dve.wait_ge(ph["xb"], t + 1)
                        dve.tensor_tensor(X[:, t, :], at(f"o{t}")[:, :], X[:, t, :], ALU.add)\
                            .then_inc(ph["x_out"], 1)
                        dve.wait_ge(ph["x_out"], t + 1)

                    layernorm_vector(dve, ph, finish)

                @block.gpsimd
                def _(pool):
                    for g in range(GROUPS):
                        def low(full, hi, lo, done):
                            if g >= 1:
                                pool.wait_ge(done, 2 * g + 1)
                                pool.tensor_tensor(ph["tmp"][:, lo, :], full, ph["tmp"][:, hi, :].bitcast(F32),
                                                   ALU.subtract).then_inc(done, 1)

                        if g >= 1:
                            stacked(pool, g - 1)
                            low(q32, QH, QL, ph["q_parts"])
                            filled(pool, f"s{g - 1}")
                        else:
                            pool.memset(dk[:, SEQ - 1:SEQ], 0.0)
                        pool.wait_ge(ph["k_ready"], g + 1)
                        pool.tensor_tensor(dk[:, 0:SEQ - 1], ph["k32"][:, 1:SEQ], ph["k32"][:, 0:SEQ - 1],
                                           ALU.subtract).then_inc(ph["dk_ready"], 1)
                        pool.tensor_tensor(k2, ph["k32"][:, :], ph["k32"][:, :], ALU.mult).then_inc(ph["k2_ready"], 1)
                        low(ph["k32"][:, :], KH, KL, ph["k_parts"])
                        low(dk, DH, DL, ph["d_parts"])
                        if g == 0:
                            for t in range(TT):
                                pool.tensor_tensor(X[:, t, :], X[:, t, :], row[:, 0, :], ALU.add).then_inc(ph["xb"], 1)

        def ffn(name, load_next, turned, store_to=None):
            sems = LN_SEMS + ["n_high", "n_low", "w32", "gate_mm", "up_mm", "silu", "hid", "h_high", "h_low",
                              "down", "down_end", "scaled", "sum_pool", "sum_dve", "next_w"]
            if store_to is not None:
                sems += ["next_x", "stored", "x_moved"]
            bufs = {"N": ([P, TT, DM], F32), "nH": ([P, KT, SEQ], F32R), "nL": ([P, KT, SEQ], F32R), "wf": ([P, 3, 3, 512], F32R),
                     "sg": ([P, 2, SEQ], F32), "h32": ([P, 2, SEQ], F32), "hH": ([P, 3, SEQ], F32R),
                     "hL": ([P, 3, SEQ], F32R), "y": ([P, TT, 512], F32)}
            if store_to is not None:
                bufs |= {"xo": ([P, TT, DM], F32), "xn": ([P, TT, DM], F32)}
            with phase(name, sems, bufs) as (ph, block):
                X_out = X if store_to is None else ph["xo"]

                def on_dve(t):
                    return store_to is not None and t % 2 == 1

                def residual(eng, t):
                    eng.wait_ge(ph["scaled"], t + 1)
                    eng.tensor_tensor(X_out[:, t, :], X[:, t, :], ph["y"][:, t, :], ALU.add)\
                        .then_inc(ph["sum_dve" if on_dve(t) else "sum_pool"], 1)

                def summed(eng, t):
                    eng.wait_ge(ph["sum_dve" if on_dve(t) else "sum_pool"], sum(on_dve(u) == on_dve(t) for u in range(t + 1)))


                @block.sync
                def _(sp):
                    if store_to is not None:
                        for t in range(TT):
                            sp.dma_start(ph["xn"][:, t, :], x[store_to + 1, t * P:(t + 1) * P, :])\
                                .then_inc(ph["next_x"], 16)
                    load_next(sp, ph["next_w"])
                    if store_to is not None:
                        for t in range(TT):
                            summed(sp, t)
                            sp.dma_start(out[store_to, t * P:(t + 1) * P, :], ph["xo"][:, t, :])\
                                .then_inc(ph["stored"], 16)
                        sp.wait_ge(ph["stored"], 16 * TT)
                        sp.wait_ge(ph["next_w"], 16 * 4)
                    else:
                        sp.wait_ge(ph["next_w"], 16 * 3)

                @block.tensor
                def _(pe):
                    def up(i):
                        for j, (done, used) in enumerate(((ph["gate_mm"], ph["silu"]), (ph["up_mm"], ph["hid"]))):
                            if i >= 2:
                                pe.wait_ge(used, i - 1)
                            w = ph["wf"][:, i % 3, j, :].rearrange("p (k n) -> p k n", k=KT)
                            for k in range(KT):
                                if i == 0 and j == 0:
                                    pe.wait_ge(ph["n_low"], k + 1)
                                for part in (ph["nH"], ph["nL"]):
                                    last = pe.matmul(bank[2 * j + i % 2][:, :], w[:, k, :], part[:, k, :],
                                                     start=(k == 0 and part is ph["nH"]),
                                                     stop=(k == KT - 1 and part is ph["nL"]))
                            last.then_inc(done, 1)

                    def down(i):
                        pe.wait_ge(ph["h_low"], i + 1)
                        for t in range(TT):
                            for part in (ph["hH"], ph["hL"]):
                                last = pe.matmul(bank[4 + t][:, :], part[:, i % 3, t * P:(t + 1) * P],
                                                 ph["wf"][:, i % 3, 2, :], start=(i == 0 and part is ph["hH"]),
                                                 stop=(i == FT - 1 and part is ph["hL"]))
                            if i == FT - 1:
                                last.then_inc(ph["down_end"], 1)
                        if i < FT - 1:
                            last.then_inc(ph["down"], 1)

                    for i in range(FT):
                        pe.wait_ge(ph["w32"], i + 1)
                        up(i)
                        if i >= 1:
                            down(i - 1)
                    if store_to is not None:
                        pe.wait_ge(ph["silu"], FT)
                        pe.wait_ge(ph["hid"], FT)
                        layernorm_turn(pe, ph, 0)
                    down(FT - 1)
                    if store_to is None:
                        layernorm_turn(pe, ph, 0)

                @block.scalar
                def _(act):
                    def widen(i):
                        if i >= 3:
                            act.wait_ge(ph["down"], i - 2)
                        act.activation(ph["wf"][:, i % 3].rearrange("p m n -> p (m n)"), ffnw[:, i, :], ACT.Copy)\
                            .then_inc(ph["w32"], 1)

                    for k in range(KT):
                        act.activation(ph["nH"][:, k, :], bank[turned + k][:, :], ACT.Copy).then_inc(ph["n_high"], 1)
                        if k == 0:
                            widen(0)
                    widen(1)
                    for i in range(FT):
                        act.wait_ge(ph["gate_mm"], i + 1)
                        if i >= 2:
                            act.wait_ge(ph["hid"], i - 1)
                        act.activation(ph["sg"][:, i % 2, :], bank[i % 2][:, :], ACT.Silu,
                                       scale=c("gate_scale", i)).then_inc(ph["silu"], 1)
                        if i + 2 < FT:
                            widen(i + 2)
                        if i == 8 and store_to is not None:
                            layernorm_scalar(act, ph)
                    if store_to is None:
                        layernorm_scalar(act, ph)
                    else:
                        for t in range(TT):
                            summed(act, t)
                            act.activation(X[:, t, :], ph["xn"][:, t, :], ACT.Copy).then_inc(ph["x_moved"], 1)

                @block.vector
                def _(dve):
                    for k in range(KT):
                        dve.wait_ge(ph["n_high"], k + 1)
                        dve.tensor_tensor(ph["nL"][:, k, :], bank[turned + k][:, :], ph["nH"][:, k, :].bitcast(F32),
                                          ALU.subtract).then_inc(ph["n_low"], 1)
                    for i in range(FT):
                        dve.wait_ge(ph["up_mm"], i + 1)
                        dve.wait_ge(ph["silu"], i + 1)
                        dve.scalar_tensor_tensor(out=ph["h32"][:, i % 2, :], in0=bank[2 + i % 2][:, :],
                                                 scalar=c("up_scale", i), in1=ph["sg"][:, i % 2, :],
                                                 op0=ALU.mult, op1=ALU.mult).then_inc(ph["hid"], 1)
                        dve.wait_ge(ph["hid"], i + 1)
                        if i >= 3:
                            dve.wait_ge(ph["down"], i - 2)
                        dve.tensor_copy(ph["hH"][:, i % 3, :], ph["h32"][:, i % 2, :]).then_inc(ph["h_high"], 1)
                        dve.wait_ge(ph["h_high"], i + 1)
                        dve.tensor_tensor(ph["hL"][:, i % 3, :], ph["h32"][:, i % 2, :],
                                          ph["hH"][:, i % 3, :].bitcast(F32), ALU.subtract).then_inc(ph["h_low"], 1)
                        if store_to is not None and 3 <= i < 3 + TT:
                            if i == 3:
                                dve.wait_ge(ph["next_x"], 16 * TT)
                            token_stats(dve, ph, i - 3, ph["xn"])
                        if store_to is not None and i == 9:
                            for t in range(TT):
                                normalise(dve, ph, t, ph["xn"])

                    def scale_down(t):
                        dve.wait_ge(ph["down_end"], t + 1)
                        dve.tensor_tensor(ph["y"][:, t, :], bank[4 + t][:, :], row[:, 1, :], ALU.mult)\
                            .then_inc(ph["scaled"], 1)

                    def finish(t):
                        if t + 2 < TT:
                            scale_down(t + 2)
                        summed(dve, t)

                    scale_down(0)
                    scale_down(1)
                    if store_to is None:
                        layernorm_vector(dve, ph, finish)
                    else:
                        residual(dve, 1)
                        scale_down(2)
                        scale_down(3)
                        residual(dve, 3)

                @block.gpsimd
                def _(pool):
                    for t in range(TT):
                        if not on_dve(t):
                            residual(pool, t)

        def mixer():
            sems = LN_SEMS + ["n_high", "n_low", "w_high", "w_low", "o_high", "o_low", "cb_high", "cb_low", "in_mm",
                              "gate_mm", "pads", "proj", "taps", "convd", "sig", "act_x", "gate_chain", "gated",
                              "dt_w", "dt_mm", "e_chain", "bounded", "relu", "dt", "decay", "drive", "scan",
                              "y", "comb", "out_mm", "out_end", "x_out"]
            NW, NCB = 3, 3
            bufs = {"N": ([P, TT, DM], F32), "nH": ([P, KT, SEQ], F32R), "nL": ([P, KT, SEQ], F32R),
                     "wH": ([P, NW, KT * P], F32R), "wL": ([P, NW, KT * P], F32R),
                     "oH": ([P, 2, DM], F32R), "oL": ([P, 2, DM], F32R),
                     "cbH": ([P, NCB, SEQ], F32R), "cbL": ([P, NCB, SEQ], F32R),
                     "pj": ([P, 2, SEQ + DCONV - 1], F32), "cv": ([P, 2, SEQ], F32),
                     "sg": ([P, 2, SEQ], F32), "Xs": ([P, MT, SEQ], F32), "gate": ([P, 2, SEQ], F32),
                     "rl": ([P, 2, SEQ], F32), "dtv": ([P, 2, SEQ], F32),
                     "cb": ([P, 2, SEQ], F32),
                     "dtw": ([P, MT, P], F32)}
            with phase("mix", sems, bufs) as (ph, block):
                ea, el = ph["N"][:, 0:2, :], ph["N"][:, 2:4, :]
                drv, dec, st = ph["pj"][:, :, 0:SEQ], ph["sg"], ph["cv"]

                def weights(u):
                    return (mix_in if u < MT else mix_gate)[:, :, u % MT * P:(u % MT + 1) * P]

                def by_k(part, u):
                    return part[:, u % NW, :].rearrange("p (k n) -> p k n", k=KT)

                @block.tensor
                def _(pe):
                    def project(u, to, done):
                        pe.wait_ge(ph["w_low"], u + 1)
                        wH, wL = by_k(ph["wH"], u), by_k(ph["wL"], u)
                        for k in range(KT):
                            if u == 0:
                                pe.wait_ge(ph["n_low"], k + 1)
                            for w, n in ((wH, ph["nH"]), (wL, ph["nH"]), (wH, ph["nL"])):
                                last = pe.matmul(to[:, :], w[:, k, :], n[:, k, :],
                                                 start=(k == 0 and w is wH and n is ph["nH"]),
                                                 stop=(k == KT - 1 and n is ph["nL"]))
                        last.then_inc(done, 1)

                    def gate(j):
                        if j >= 2:
                            pe.wait_ge(ph["gate_chain"], 2 * (j - 2) + 1)
                        project(MT + j, bank[2 + j % 2], ph["gate_mm"])

                    def dt_rows(j):
                        pe.wait_ge(ph["act_x"], j + 1)
                        if j < 2:
                            pe.wait_ge(ph["proj"], MT)
                        else:
                            pe.wait_ge(ph["relu"], j - 1)
                        pe.matmul(bank[j % 2][:, :], ph["dtw"][:, j, :], ph["Xs"][:, j, :], start=True, stop=True)\
                            .then_inc(ph["dt_mm"], 1)

                    def project_out(j):
                        pe.wait_ge(ph["cb_low"], j + 1)
                        pe.wait_ge(ph["o_low"], j + 1)
                        for t in range(TT):
                            for x, w in (("cbH", "oH"), ("cbH", "oL"), ("cbL", "oH")):
                                last = pe.matmul(bank[4 + t][:, :], ph[x][:, j % NCB, t * P:(t + 1) * P],
                                                 ph[w][:, j % 2, :], start=(j == 0 and (x, w) == ("cbH", "oH")),
                                                 stop=(j == MT - 1 and x == "cbL"))
                            if j == MT - 1:
                                last.then_inc(ph["out_end"], 1)
                        if j < MT - 1:
                            last.then_inc(ph["out_mm"], 1)

                    for j in range(MT):
                        if j >= 2:
                            pe.wait_ge(ph["proj"], j - 1)
                        project(j, bank[j % 2], ph["in_mm"])
                    gate(0)
                    pe.wait_ge(ph["dt_w"], MT)
                    dt_rows(0)
                    dt_rows(1)
                    gate(1)
                    dt_rows(2)
                    for j in range(MT):
                        if j + 3 < MT:
                            dt_rows(j + 3)
                        project_out(j)
                        if j + 2 < MT:
                            gate(j + 2)
                    layernorm_turn(pe, ph, 0)

                @block.scalar
                def _(act):
                    def split_high(u):
                        used = u - NW + 1
                        if used > 0:
                            act.wait_ge(ph["in_mm"], min(used, MT))
                        if used > MT:
                            act.wait_ge(ph["gate_mm"], used - MT)
                        act.activation(by_k(ph["wH"], u), weights(u), ACT.Copy).then_inc(ph["w_high"], 1)

                    def out_high(j):
                        if j >= 2:
                            act.wait_ge(ph["out_mm"], j - 1)
                        act.activation(ph["oH"][:, j % 2, :], mix_out[:, j, :], ACT.Copy).then_inc(ph["o_high"], 1)

                    split_high(0)
                    for k in range(KT):
                        act.activation(ph["nH"][:, k, :], bank[k][:, :], ACT.Copy).then_inc(ph["n_high"], 1)
                    for u in range(1, NW):
                        split_high(u)

                    def silu_gate(j):
                        act.wait_ge(ph["convd"], j + 1)
                        if j >= 2:
                            act.wait_ge(ph["act_x"], j - 1)
                        act.activation(ph["sg"][:, j % 2, :], ph["cv"][:, j % 2, :], ACT.Sigmoid).then_inc(ph["sig"], 1)

                    for j in range(MT):
                        act.wait_ge(ph["in_mm"], j + 1)
                        act.wait_ge(ph["pads"], 2)
                        if j >= 2:
                            act.wait_ge(ph["convd"], j - 1)
                        act.activation(ph["pj"][:, j % 2, DCONV - 1:], bank[j % 2][:, :], ACT.Copy)\
                            .then_inc(ph["proj"], 1)
                        split_high(j + NW)
                        if j >= 1:
                            silu_gate(j - 1)
                    out_high(0)
                    silu_gate(MT - 1)
                    act.preload_act_table_set("natural_log_exp_and_others")

                    def bounded(j):
                        s = j % 2
                        act.wait_ge(ph["dt_mm"], j + 1)
                        act.activation(ea[:, s, :], bank[s][:, :], ACT.Abs, bias=c("dt_b", j))\
                            .then_inc(ph["e_chain"], 1)
                        act.wait_ge(ph["e_chain"], 2 * j + 1)
                        act.activation(ea[:, s, :], ea[:, s, :], ACT.Exp, scale=-1.0).then_inc(ph["e_chain"], 1)
                        act.wait_ge(ph["e_chain"], 2 * j + 2)
                        if j >= 2:
                            act.wait_ge(ph["dt"], j - 1)
                        act.activation(el[:, s, :], ea[:, s, :], ACT.Ln, bias=1.0).then_inc(ph["bounded"], 1)

                    def decay(j):
                        s = j % 2
                        if j == 0:
                            act.wait_ge(ph["act_x"], MT)
                        act.wait_ge(ph["dt"], j + 1)
                        if j >= 2:
                            act.wait_ge(ph["scan"], j - 1)
                        act.activation(dec[:, s, :], ph["dtv"][:, s, :], ACT.Exp, scale=negA[:, j:j + 1])\
                            .then_inc(ph["decay"], 1)

                    def gate(j):
                        g = ph["gate"][:, j % 2, :]
                        act.wait_ge(ph["gate_mm"], j + 1)
                        if j >= 2:
                            act.wait_ge(ph["comb"], j - 1)
                        act.activation(g, bank[2 + j % 2][:, :], ACT.Exp, scale=-1.0).then_inc(ph["gate_chain"], 1)
                        act.wait_ge(ph["gate_chain"], 2 * j + 1)
                        act.activation(g, g, ACT.Ln, bias=1.0).then_inc(ph["gate_chain"], 1)
                        act.wait_ge(ph["gate_chain"], 2 * j + 2)
                        act.activation(g, g, ACT.Exp, scale=-1.0).then_inc(ph["gated"], 1)

                    bounded(0)
                    for j in range(MT):
                        if j + 1 < MT:
                            bounded(j + 1)
                        decay(j)
                        gate(j)
                        if j + 1 < MT:
                            out_high(j + 1)
                        if j + NW < MT:
                            split_high(MT + j + NW)
                    layernorm_scalar(act, ph)

                @block.vector
                def _(dve):
                    for k in range(KT):
                        dve.wait_ge(ph["n_high"], k + 1)
                        dve.tensor_tensor(ph["nL"][:, k, :], bank[k][:, :], ph["nH"][:, k, :].bitcast(F32),
                                          ALU.subtract).then_inc(ph["n_low"], 1)
                    n = 0
                    for j in range(MT):
                        s = j % 2
                        dve.wait_ge(ph["proj"], j + 1)
                        if j >= 2:
                            dve.wait_ge(ph["act_x"], j - 1)
                        cv = ph["cv"][:, s, :]
                        w = COLS["conv_w"] + j * DCONV
                        dve.tensor_scalar(cv, ph["pj"][:, s, 0:SEQ], col[:, w:w + 1], c("conv_b", j),
                                          ALU.mult, ALU.add).then_inc(ph["taps"], 1)
                        n += 1
                        for k in range(1, DCONV):
                            dve.wait_ge(ph["taps"], n)
                            last = dve.scalar_tensor_tensor(out=cv, in0=ph["pj"][:, s, k:k + SEQ],
                                                            scalar=col[:, w + k:w + k + 1], in1=cv,
                                                            op0=ALU.mult, op1=ALU.add)
                            if k < DCONV - 1:
                                last.then_inc(ph["taps"], 1)
                                n += 1
                        last.then_inc(ph["convd"], 1)

                    def time_step(j):
                        s = j % 2
                        dve.wait_ge(ph["e_chain"], 2 * j + 1)
                        if j >= 2:
                            dve.wait_ge(ph["dt"], j - 1)
                        dve.tensor_scalar(ph["rl"][:, s, :], bank[s][:, :], c("dt_b", j), 0.0, ALU.add, ALU.max)\
                            .then_inc(ph["relu"], 1)
                        dve.wait_ge(ph["relu"], j + 1)
                        dve.wait_ge(ph["bounded"], j + 1)
                        if j >= 2:
                            dve.wait_ge(ph["decay"], j - 1)
                        dve.tensor_tensor(ph["dtv"][:, s, :], ph["rl"][:, s, :], el[:, s, :], ALU.add)\
                            .then_inc(ph["dt"], 1)
                        dve.wait_ge(ph["dt"], j + 1)
                        dve.scalar_tensor_tensor(out=drv[:, s, :], in0=ph["dtv"][:, s, :], scalar=bc[:, j:j + 1],
                                                 in1=ph["Xs"][:, j, :], op0=ALU.mult, op1=ALU.mult)\
                            .then_inc(ph["drive"], 1)

                    time_step(0)
                    for j in range(MT):
                        s = j % 2
                        if j + 1 < MT:
                            time_step(j + 1)
                        dve.wait_ge(ph["drive"], j + 1)
                        dve.wait_ge(ph["decay"], j + 1)
                        if j == 0:
                            dve.wait_ge(ph["act_x"], MT)
                        dve.tensor_tensor_scan(st[:, s, :], dec[:, s, :], drv[:, s, :], 0.0,
                                               ALU.mult, ALU.add).then_inc(ph["scan"], 1)
                        dve.wait_ge(ph["scan"], j + 1)
                        dve.scalar_tensor_tensor(out=st[:, s, :], in0=ph["Xs"][:, j, :], scalar=c("Dp", j),
                                                 in1=st[:, s, :], op0=ALU.mult, op1=ALU.add)\
                            .then_inc(ph["y"], 1)
                        dve.wait_ge(ph["y"], j + 1)
                        dve.wait_ge(ph["gated"], j + 1)
                        if j >= 2:
                            dve.wait_ge(ph["cb_low"], j - 1)
                        dve.tensor_tensor(ph["cb"][:, s, :], st[:, s, :], ph["gate"][:, s, :], ALU.mult)\
                            .then_inc(ph["comb"], 1)
                        dve.wait_ge(ph["comb"], j + 1)
                        if j >= NCB:
                            dve.wait_ge(ph["out_mm"], j - NCB + 1)
                        dve.tensor_copy(ph["cbH"][:, j % NCB, :], ph["cb"][:, s, :]).then_inc(ph["cb_high"], 1)

                    def finish(t):
                        dve.wait_ge(ph["out_end"], t + 1)
                        dve.tensor_tensor(X[:, t, :], bank[4 + t][:, :], X[:, t, :], ALU.add)\
                            .then_inc(ph["x_out"], 1)
                        dve.wait_ge(ph["x_out"], t + 1)

                    layernorm_vector(dve, ph, finish)

                @block.gpsimd
                def _(pool):
                    def split_low(u):
                        pool.wait_ge(ph["w_high"], u + 1)
                        pool.tensor_tensor(by_k(ph["wL"], u), weights(u), by_k(ph["wH"], u).bitcast(F32),
                                           ALU.subtract).then_inc(ph["w_low"], 1)

                    def out_low(j):
                        pool.wait_ge(ph["o_high"], j + 1)
                        pool.tensor_tensor(ph["oL"][:, j % 2, :], mix_out[:, j, :], ph["oH"][:, j % 2, :].bitcast(F32),
                                           ALU.subtract).then_inc(ph["o_low"], 1)

                    for s in range(2):
                        pool.memset(ph["pj"][:, s, 0:DCONV - 1], 0.0).then_inc(ph["pads"], 1)
                    for u in range(NW):
                        split_low(u)
                    for j in range(MT):
                        pool.tensor_scalar(ph["dtw"][:, j, :], hmask[:, :], c("dt_w", j), None, ALU.mult)\
                            .then_inc(ph["dt_w"], 1)
                    for j in range(MT):
                        split_low(j + NW)
                        pool.wait_ge(ph["sig"], j + 1)
                        pool.tensor_tensor(ph["Xs"][:, j, :], ph["cv"][:, j % 2, :], ph["sg"][:, j % 2, :], ALU.mult)\
                            .then_inc(ph["act_x"], 1)
                    out_low(0)
                    for j in range(MT):
                        pool.wait_ge(ph["cb_high"], j + 1)
                        pool.tensor_tensor(ph["cbL"][:, j % NCB, :], ph["cb"][:, j % 2, :],
                                           ph["cbH"][:, j % NCB, :].bitcast(F32), ALU.subtract)\
                            .then_inc(ph["cb_low"], 1)
                        if j + 1 < MT:
                            out_low(j + 1)
                        if j + NW < MT:
                            split_low(MT + j + NW)

        setup()
        with nc.Fori(0, BATCH) as b:
            attention()
            ffn("ffn1", load_mix_weights, turned=4)
            mixer()
            ffn("ffn2", load_att_weights, turned=0, store_to=b)


def kernel(**inputs):
    import numpy as np
    import concourse.bacc as bacc
    from concourse.bass_utils import run_bass_kernel_spmd

    a = {k: np.asarray(v) for k, v in inputs.items()}
    A, B, C = "L0_attn_a_", "L0_attn_b_", "L0_ffn_"

    def columns(v, width):
        return v.reshape(width, P).T

    def feature_first(w):
        return w.reshape((GROUPS, HG, HD) + w.shape[1:]).swapaxes(1, 2).reshape(w.shape)

    conv_w = a[B + "conv_w"].reshape(MT, P, DCONV).transpose(1, 0, 2).reshape(P, MT * DCONV)
    gates = [a[A + g + "_gate"] for g in ("truth", "balance", "order", "justice", "harmony")]
    cols = np.concatenate(
        [columns(feature_first(a[A + "bq"]), KT), columns(feature_first(a[A + "bk"]), KT),
         columns(a[C + "gate_scale"], FT), columns(a[C + "up_scale"], FT), conv_w,
         columns(a[B + "conv_b"], MT), columns(a[B + "dt_w"], MT),
         columns(np.repeat(a[B + "dt_b"], HDIM), MT)]
        + [columns(a[B + n], MT) for n in ("A_log", "Bp", "Cp", "Dp")]
        + [np.broadcast_to(g, (P, 1)) for g in gates], axis=1)
    rows = np.broadcast_to(np.stack([a[A + "bo"], a[C + "down_scale"], a[A + "bv"]]), (P, 3, DM))
    i = np.arange(P)
    arrays = {
        "x": np.concatenate([a[A + "hidden_states"], a[A + "hidden_states"][:1]]),
        "wq": feature_first(a[A + "Wq"]).T, "wk": feature_first(a[A + "Wk"]).T, "wv": a[A + "Wv"].T, "wo": a[A + "Wo"].T,
        "w_gate": a[C + "gate_w"], "w_up": a[C + "up_w"], "w_down": a[C + "down_w"],
        "w_in": a[B + "in_proj_w"].T, "w_mg": a[B + "gate_proj_w"].T, "w_out": a[B + "out_proj_w"].T,
        "cols": cols, "rows": rows,
        "identity": np.eye(P, dtype=np.float32),
        "head_mask": (i[:, None] // HDIM == i[None, :] // HDIM).astype(np.float32),
        "group_mask": (i[:, None] % HG == np.arange(HG)[None, :]).astype(np.float32),
        "key_pos": np.tile((np.arange(SEQ) * ORDER_STEP).astype(np.float32), (ROW_TERMS, 1)),
    }
    arrays = {k: np.ascontiguousarray(v) for k, v in arrays.items()}
    nc = bacc.Bacc("TRN2", target_bir_lowering=False, num_devices=1)
    args = [nc.dram_tensor(k, v.shape, mybir.dt.from_np(v.dtype), kind="ExternalInput").ap()
            for k, v in arrays.items()]
    out = nc.dram_tensor("out", (BATCH, SEQ, DM), F32, kind="ExternalOutput").ap()
    hybrid_layers(nc, *args, out)
    r = run_bass_kernel_spmd(nc, [arrays], core_ids=[0])
    return r.results[0]["out"]
```
